# Optimizing a Trainium2 kernel written in Bass

```python
import numpy as np
import jax
import jax.numpy as jnp

def _softmax(x, axis=-1):
    return jax.nn.softmax(x, axis=axis)

def _gelu(x):
    return jax.nn.gelu(x, approximate=True)

def _silu(x):
    return jax.nn.silu(x)

def _sigmoid(x):
    return jax.nn.sigmoid(x)

def _layernorm(x, axis=-1, eps=1e-05):
    m = jnp.mean(x, axis=axis, keepdims=True)
    v = jnp.var(x, axis=axis, keepdims=True)
    return (x - m) / jnp.sqrt(v + eps)

def _scatter_add(tgt, idx, src, axis=0):
    return tgt.at[idx].add(src)

def _segment_sum(src, seg, n):
    return jax.ops.segment_sum(src, seg, n)
kernel_name = 'mk_prb_d2_jaxref_r8_21f731'

def setup_inputs(seed: int=0):
    np.random.seed(seed)
    _w = jnp.asarray

    def _L0_attn_setup():
        import jax, jax.numpy as jnp
        import numpy as np
        from math import sqrt
        NUM_HEADS = 16
        NUM_KV_HEADS = 4
        ROPE_BASE = 10000.0

        def _rope_cos_sin(seq_len, head_dim, dtype):
            inv_freq = 1.0 / ROPE_BASE ** (jnp.arange(0, head_dim, 2, dtype=jnp.float32) / head_dim)
            pos = jnp.arange(seq_len, dtype=jnp.float32)
            freqs = pos[:, None] * inv_freq[None, :]
            emb = jnp.concatenate([freqs, freqs], axis=-1)
            return (jnp.cos(emb).astype(dtype), jnp.sin(emb).astype(dtype))

        def _apply_rope(t, cos, sin):
            d2 = t.shape[-1] // 2
            rot = jnp.concatenate([-t[..., d2:], t[..., :d2]], axis=-1)
            return t * cos[None, None, :, :] + rot * sin[None, None, :, :]
        key = jax.random.key(seed)
        ks = jax.random.split(key, 9)
        B, S, E = (4, 256, 256)
        KV_DIM = NUM_KV_HEADS * (E // NUM_HEADS)
        s = 0.02
        return {'x': jax.random.normal(ks[0], (B, S, E), jnp.float32), 'wq': jax.random.normal(ks[1], (E, E), jnp.float32) * s, 'bq': jnp.zeros((E,), jnp.float32), 'wk': jax.random.normal(ks[2], (KV_DIM, E), jnp.float32) * s, 'bk': jnp.zeros((KV_DIM,), jnp.float32), 'wv': jax.random.normal(ks[3], (KV_DIM, E), jnp.float32) * s, 'bv': jnp.zeros((KV_DIM,), jnp.float32), 'wo': jax.random.normal(ks[4], (E, E), jnp.float32) * s, 'bo': jnp.zeros((E,), jnp.float32)}
    _L0_attn_in = _L0_attn_setup()

    def _L0_ffn_setup():
        import jax, jax.numpy as jnp
        import numpy as np

        def binarize_weight(w):
            alpha = jnp.mean(jnp.abs(w), axis=tuple(range(1, w.ndim)), keepdims=True)
            bw = jnp.where(w >= 0, 1.0, -1.0) * alpha
            return jax.lax.stop_gradient(bw - w) + w
        key = jax.random.key(seed)
        k1, k2, k3 = jax.random.split(key, 3)
        in_features, out_features = (256, 256)
        x = jax.random.normal(k1, (8, 256, in_features), dtype=jnp.float32)
        std = np.sqrt(2.0 / out_features).astype(np.float32)
        weight = jax.random.normal(k2, (out_features, in_features), dtype=jnp.float32) * std
        bias = jax.random.normal(k3, (out_features,), dtype=jnp.float32) * 0.01
        return {'x': x, 'weight': weight, 'bias': bias}
    _L0_ffn_in = _L0_ffn_setup()

    def _L1_attn_setup():
        import jax, jax.numpy as jnp
        import numpy as np
        EPS = 1.1920929e-07

        def _rms(x):
            return x * jax.lax.rsqrt(jnp.mean(x * x, axis=-1, keepdims=True) + EPS)
        key = jax.random.key(seed)
        k0, k1, k2, k3 = jax.random.split(key, 4)
        B, S, D, DFF = (4, 256, 256, 1024)
        x = jax.random.normal(k0, (B, S, D), dtype=jnp.float32)
        w_qkv = jax.random.normal(k1, (3 * D, D), dtype=jnp.float32) * 0.02
        w_swiglu = jax.random.normal(k2, (2 * DFF, D), dtype=jnp.float32) * 0.02
        w_out = jax.random.normal(k3, (D, DFF), dtype=jnp.float32) * 0.02
        return {'x': x, 'w_qkv': w_qkv, 'w_swiglu': w_swiglu, 'w_out': w_out}
    _L1_attn_in = _L1_attn_setup()

    def _L1_ffn_setup():
        import jax, jax.numpy as jnp
        import numpy as np
        BLOCK_SIZE = 32
        HIDDEN_SIZE = 256
        MLP_DIM = 2048
        NVFP4_LUT = jnp.array([0.0, 0.5, 1.0, 1.5, 2.0, 3.0, 4.0, 6.0, 0.0, -0.5, -1.0, -1.5, -2.0, -3.0, -4.0, -6.0], dtype=jnp.float32)

        def dequant_nvfp4(W_packed, scales, block=BLOCK_SIZE):
            N = W_packed.shape[0]
            low = W_packed & 15
            high = W_packed >> 4 & 15
            idx = jnp.stack([low, high], axis=-1).reshape(N, -1)
            vals = NVFP4_LUT[idx]
            K = vals.shape[1]
            vals = vals.reshape(N, K // block, block) * scales[:, :, None]
            return vals.reshape(N, K)
        key = jax.random.key(seed)
        ks = jax.random.split(key, 7)
        x = jax.random.normal(ks[0], (4, 32, HIDDEN_SIZE), dtype=jnp.float32)
        gate_W_packed = jax.random.randint(ks[1], (MLP_DIM, HIDDEN_SIZE // 2), 0, 32, dtype=jnp.int32)
        gate_scales = jax.random.uniform(ks[2], (MLP_DIM, HIDDEN_SIZE // BLOCK_SIZE), dtype=jnp.float32) * 0.1 + 0.001
        up_W_packed = jax.random.randint(ks[3], (MLP_DIM, HIDDEN_SIZE // 2), 0, 32, dtype=jnp.int32)
        up_scales = jax.random.uniform(ks[4], (MLP_DIM, HIDDEN_SIZE // BLOCK_SIZE), dtype=jnp.float32) * 0.1 + 0.001
        down_W_packed = jax.random.randint(ks[5], (HIDDEN_SIZE, MLP_DIM // 2), 0, 32, dtype=jnp.int32)
        down_scales = jax.random.uniform(ks[6], (HIDDEN_SIZE, MLP_DIM // BLOCK_SIZE), dtype=jnp.float32) * 0.1 + 0.001
        return {'x': x, 'gate_W_packed': gate_W_packed, 'gate_scales': gate_scales, 'up_W_packed': up_W_packed, 'up_scales': up_scales, 'down_W_packed': down_W_packed, 'down_scales': down_scales}
    _L1_ffn_in = _L1_ffn_setup()
    _d = {'L0_attn_x': _L0_attn_in['x'], 'L0_attn_wq': _L0_attn_in['wq'], 'L0_attn_bq': _L0_attn_in['bq'], 'L0_attn_wk': _L0_attn_in['wk'], 'L0_attn_bk': _L0_attn_in['bk'], 'L0_attn_wv': _L0_attn_in['wv'], 'L0_attn_bv': _L0_attn_in['bv'], 'L0_attn_wo': _L0_attn_in['wo'], 'L0_attn_bo': _L0_attn_in['bo'], 'L0_ffn_weight': _L0_ffn_in['weight'], 'L0_ffn_bias': _L0_ffn_in['bias'], 'L1_attn_w_qkv': _L1_attn_in['w_qkv'], 'L1_attn_w_swiglu': _L1_attn_in['w_swiglu'], 'L1_attn_w_out': _L1_attn_in['w_out'], 'L1_ffn_gate_W_packed': _L1_ffn_in['gate_W_packed'], 'L1_ffn_gate_scales': _L1_ffn_in['gate_scales'], 'L1_ffn_up_W_packed': _L1_ffn_in['up_W_packed'], 'L1_ffn_up_scales': _L1_ffn_in['up_scales'], 'L1_ffn_down_W_packed': _L1_ffn_in['down_W_packed'], 'L1_ffn_down_scales': _L1_ffn_in['down_scales']}
    _x0 = _d['L0_attn_x']
    _d['L0_attn_x'] = jax.random.normal(jax.random.fold_in(jax.random.key(seed), 1), (4, 1024, 256), dtype=_x0.dtype)
    del _x0
    return _d

def reference(L0_attn_x, L0_attn_wq, L0_attn_bq, L0_attn_wk, L0_attn_bk, L0_attn_wv, L0_attn_bv, L0_attn_wo, L0_attn_bo, L0_ffn_weight, L0_ffn_bias, L1_attn_w_qkv, L1_attn_w_swiglu, L1_attn_w_out, L1_ffn_gate_W_packed, L1_ffn_gate_scales, L1_ffn_up_W_packed, L1_ffn_up_scales, L1_ffn_down_W_packed, L1_ffn_down_scales):

    def _L0_attn_ref(x, wq, bq, wk, bk, wv, bv, wo, bo):
        import jax, jax.numpy as jnp
        import numpy as np
        from math import sqrt
        NUM_HEADS = 16
        NUM_KV_HEADS = 4
        ROPE_BASE = 10000.0

        def _rope_cos_sin(seq_len, head_dim, dtype):
            inv_freq = 1.0 / ROPE_BASE ** (jnp.arange(0, head_dim, 2, dtype=jnp.float32) / head_dim)
            pos = jnp.arange(seq_len, dtype=jnp.float32)
            freqs = pos[:, None] * inv_freq[None, :]
            emb = jnp.concatenate([freqs, freqs], axis=-1)
            return (jnp.cos(emb).astype(dtype), jnp.sin(emb).astype(dtype))

        def _apply_rope(t, cos, sin):
            d2 = t.shape[-1] // 2
            rot = jnp.concatenate([-t[..., d2:], t[..., :d2]], axis=-1)
            return t * cos[None, None, :, :] + rot * sin[None, None, :, :]
        B, S, E = x.shape
        H, KV = (NUM_HEADS, NUM_KV_HEADS)
        D = E // H
        G = H // KV
        q = (x @ wq.T + bq).reshape(B, S, H, D).transpose(0, 2, 1, 3)
        k = (x @ wk.T + bk).reshape(B, S, KV, D).transpose(0, 2, 1, 3)
        v = (x @ wv.T + bv).reshape(B, S, KV, D).transpose(0, 2, 1, 3)
        cos, sin = _rope_cos_sin(S, D, x.dtype)
        q = _apply_rope(q, cos, sin)
        k = _apply_rope(k, cos, sin)
        k = jnp.repeat(k, G, axis=1)
        v = jnp.repeat(v, G, axis=1)
        scores = jnp.einsum('bhqd,bhkd->bhqk', q, k)
        causal = jnp.triu(jnp.ones((S, S), dtype=bool), k=1)
        scores = jnp.where(causal[None, None, :, :], -jnp.inf, scores)
        attn = jax.nn.softmax(scores / sqrt(D), axis=-1)
        out = jnp.einsum('bhqk,bhkd->bhqd', attn, v)
        out = out.transpose(0, 2, 1, 3).reshape(B, S, E)
        return out @ wo.T + bo

    def _L0_ffn_ref(x, weight, bias):
        import jax, jax.numpy as jnp
        import numpy as np

        def binarize_weight(w):
            alpha = jnp.mean(jnp.abs(w), axis=tuple(range(1, w.ndim)), keepdims=True)
            bw = jnp.where(w >= 0, 1.0, -1.0) * alpha
            return jax.lax.stop_gradient(bw - w) + w
        bw = binarize_weight(weight)
        return jnp.einsum('bsi,oi->bso', x, bw) + bias

    def _L1_attn_ref(x, w_qkv, w_swiglu, w_out):
        import jax, jax.numpy as jnp
        import numpy as np
        EPS = 1.1920929e-07

        def _rms(x):
            return x * jax.lax.rsqrt(jnp.mean(x * x, axis=-1, keepdims=True) + EPS)
        qkv = _rms(x) @ w_qkv.T
        q, k, v = jnp.split(qkv, 3, axis=-1)
        q = _rms(q)
        k = _rms(k)
        w = jnp.exp(k)
        kv_cum = jnp.cumsum(w * v, axis=1)
        w_cum = jnp.cumsum(w, axis=1)
        y = jax.nn.sigmoid(q) * (kv_cum / (w_cum + 1e-06))
        uv = y @ w_swiglu.T
        u, g = jnp.split(uv, 2, axis=-1)
        return x + u * jax.nn.silu(g) @ w_out.T

    def _L1_ffn_ref(x, gate_W_packed, gate_scales, up_W_packed, up_scales, down_W_packed, down_scales):
        import jax, jax.numpy as jnp
        import numpy as np
        BLOCK_SIZE = 32
        HIDDEN_SIZE = 256
        MLP_DIM = 2048
        NVFP4_LUT = jnp.array([0.0, 0.5, 1.0, 1.5, 2.0, 3.0, 4.0, 6.0, 0.0, -0.5, -1.0, -1.5, -2.0, -3.0, -4.0, -6.0], dtype=jnp.float32)

        def dequant_nvfp4(W_packed, scales, block=BLOCK_SIZE):
            N = W_packed.shape[0]
            low = W_packed & 15
            high = W_packed >> 4 & 15
            idx = jnp.stack([low, high], axis=-1).reshape(N, -1)
            vals = NVFP4_LUT[idx]
            K = vals.shape[1]
            vals = vals.reshape(N, K // block, block) * scales[:, :, None]
            return vals.reshape(N, K)
        B, S, H = x.shape
        xt = x.reshape(B * S, H)
        Wg = dequant_nvfp4(gate_W_packed, gate_scales)
        Wu = dequant_nvfp4(up_W_packed, up_scales)
        Wd = dequant_nvfp4(down_W_packed, down_scales)
        gate = jnp.einsum('th,nh->tn', xt, Wg)
        up = jnp.einsum('th,nh->tn', xt, Wu)
        gelu = jnp.tanh(0.7978845608028654 * (gate + 0.044715 * gate ** 3)) * gate * 0.5 + gate * 0.5
        inter = gelu * up
        out = jnp.einsum('tn,hn->th', inter, Wd)
        return out.reshape(B, S, H)
    x = L0_attn_x
    xn = _layernorm(x, axis=-1)
    x = x + _L0_attn_ref(xn, L0_attn_wq, L0_attn_bq, L0_attn_wk, L0_attn_bk, L0_attn_wv, L0_attn_bv, L0_attn_wo, L0_attn_bo) + _L0_ffn_ref(xn, L0_ffn_weight, L0_ffn_bias)
    xn = _layernorm(x, axis=-1)
    x = x + _L1_attn_ref(xn, L1_attn_w_qkv, L1_attn_w_swiglu, L1_attn_w_out) + _L1_ffn_ref(xn, L1_ffn_gate_W_packed, L1_ffn_gate_scales, L1_ffn_up_W_packed, L1_ffn_up_scales, L1_ffn_down_W_packed, L1_ffn_down_scales)
    return x

_drawn_inputs = setup_inputs


def setup_inputs(seed=0):
    import zlib

    import numpy as np

    out = dict(_drawn_inputs(seed))
    spreads = {'L0_attn_bq': (0.0, 0.8),
     'L0_attn_bk': (0.0, 0.8),
     'L0_attn_bv': (0.0, 0.288),
     'L0_attn_bo': (0.0, 0.1)}
    factors = {'L0_attn_wq': 8.0,
     'L0_attn_wk': 8.0,
     'L0_attn_wv': 6.659,
     'L0_ffn_bias': 6.116,
     'L1_attn_w_qkv': 8.0,
     'L1_attn_w_swiglu': 8.0,
     'L1_attn_w_out': 8.0}
    for name, (base, spread) in spreads.items():
        noise = np.random.default_rng([zlib.crc32(name.encode()), seed]).standard_normal(out[name].shape)
        drawn = base * np.exp(spread * noise) if base else spread * noise
        out[name] = jnp.asarray(drawn.astype(out[name].dtype))
    for name, factor in factors.items():
        out[name] = (out[name] * factor).astype(out[name].dtype)
    return out
```

```python
from contextlib import ExitStack

import numpy as np

import concourse.bass as bass
from concourse import mybir

ALU = mybir.AluOpType
ACT = mybir.ActivationFunctionType
AX_X = mybir.AxisListType.X
F32 = mybir.dt.float32
F32R = mybir.dt.float32r
BF16 = mybir.dt.bfloat16
I32 = mybir.dt.int32

P = 128
B, S, E = 4, 1024, 256
KE = E // P
H, KV, D = 16, 4, 16
G = H // KV
TT = S // P
CW = 512
NC = S // CW
TC = CW // P
LN_EPS = 1e-5

PIECES = 3
STACK = PIECES * D
PAIR = 2 * STACK
SHIFT = PAIR
ROWS = PAIR + 2


def f32(ap):
    return ap.bitcast(F32)


def wait_alone(engine, passed, sem, value):
    engine.wait_ge(sem, value)
    engine.sem_inc(passed, 1)



W_Q = 0
W_QR = W_Q + E
W_K = W_QR + E
W_KR = W_K + 2 * KV * D
W_O = W_KR + KV * D
W_ALL0 = W_O + E
W_BIN = W_ALL0
W_ALL = W_BIN + E

ITEMS = [(c, g) for c in range(NC) for g in range(KV)]
LOOKAHEAD = 2
P_SLOTS = 3


def max_units(n):
    c, g = ITEMS[n]
    out = []
    for qt in range(TC * c, TC * c + TC):
        width = (qt + 1) * P
        for pair in range(2):
            out += [(qt, pair, k0, min(CW, width - k0)) for k0 in range(0, width, CW)]
    return out


def key_tiles(n):
    c, _ = ITEMS[n]
    return [(kt, max(0, kt - TC * c) * P, kt >= TC * c) for kt in range(TC * (c + 1))]


UNITS = [len(max_units(n)) for n in range(len(ITEMS))]
GROUPS = [len(key_tiles(n)) for n in range(len(ITEMS))]
GROUP_OF = [(n, j) for n in range(len(ITEMS)) for j in range(GROUPS[n])]
DIAGONALS = list(np.cumsum([key_tiles(n)[j][2] for n, j in GROUP_OF]))
NORM = 3
UNITS_ALL, GROUPS_ALL, DIAG_ALL = sum(UNITS), sum(GROUPS), TC * len(ITEMS)
assert GROUPS_ALL % P_SLOTS == 0 and UNITS_ALL % 2 == 0


def phase_a(nc, x, w0, w_bin, bias_cols, bias_rows, rope, x1):
    ctx = ExitStack()
    with ctx:
        def sb(name, shape, dt=F32):
            return ctx.enter_context(nc.sbuf_tensor(name, shape, dt))

        def sem(name):
            return ctx.enter_context(nc.semaphore("a_" + name))

        wh = sb("a_wh", [P, KE, W_ALL], F32R)
        wl = sb("a_wl", [P, KE, W_ALL], F32R)
        wb = sb("a_wb", [P, KE, E])
        wt = sb("a_wt", [P, KE, E])
        wabs = sb("a_wabs", [P, KE, 1])
        bcol = sb("a_bcol", [P, 6])
        brow = sb("a_brow", [P, 2, E])
        bsum = sb("a_bsum", [P, E])
        cos = sb("a_cos", [P, S])
        sin = sb("a_sin", [P, S])
        ident = sb("a_ident", [P, P])
        identb = sb("a_identb", [P, P], BF16)
        future = sb("a_future", [P, P], BF16)
        xb = sb("a_xb", [P, TT, E])
        xn = sb("a_xn", [P, TT, E])
        xr = sb("a_xr", [P, TT, E])
        stats = sb("a_stats", [P, TT, 6])
        mv = sb("a_mv", [P, TT, 2])
        rstd = sb("a_rstd", [P, TT])
        half = sb("a_half", [P, TT])
        xh = sb("a_xh", [P, KE, S], F32R)
        xl = sb("a_xl", [P, KE, S], F32R)
        qh = sb("a_qh", [P, KE, S], F32R)
        ql = sb("a_ql", [P, KE, S], F32R)
        kh = sb("a_kh", [KV * D, S], F32R)
        kl = sb("a_kl", [KV * D, S], F32R)
        vv = sb("a_vv", [P, TT, KV, 2 * D])
        qs = sb("a_qs", [P, H // 2, S], F32R)
        ks = sb("a_ks", [P, 2, KV, S], F32R)
        pr = sb("a_pr", [P, P_SLOTS, G, CW])
        mx = sb("a_mx", [P, 2, NC, TC, G])
        mm = sb("a_mm", [P, 2, TC, G])
        mt = sb("a_mt", [G, 2, CW], F32R)
        ot = sb("a_ot", [P, 2, CW])
        rc = sb("a_rc", [P, 2, CW // (2 * D)])
        nm = sb("a_nm", [P, CW])
        at = sb("a_at", [P, 2, CW])
        ps = ctx.enter_context(nc.psum_tensor("a_ps", [P, 8, CW], F32))
        BANK_S, BANK_O, BANK_X = 4, 6, 7
        t1, t2 = pr[:, 0, 0, :], pr[:, 0, 1, :]
        qf = pr[:, 1, 0:3, :]
        pr_w = pr[:, 0, :, :].rearrange("p g c -> p (g c)")[:, 0:KE * W_ALL0].rearrange("p (k n) -> p k n", k=KE)
        wabs_out = pr[:, 1, 0:KE, 0:E]
        ones = xn[0:1, :, :].rearrange("p t e -> p (t e)")[:, 0:S]
        vt = pr[:, 2, 0:NC, :].rearrange("p c t -> p (c t)")

        passed = {e: sem("passed_" + e) for e in ("pe", "dve", "pool")}
        w_in = sem("w_in")
        k_one = sem("k_one")
        w_stage = sem("w_stage")
        w_abs = sem("w_abs")
        w_bw = sem("w_bw")
        w_bt = sem("w_bt")
        w_hi = sem("w_hi")
        w_lo = sem("w_lo")
        const = sem("const")
        fixed = sem("fixed")
        x_in = sem("x_in")
        ln = sem("ln")
        ln_pool = sem("ln_pool")
        xt_ready = sem("xt_ready")
        xh_done = sem("xh_done")
        xl_done = sem("xl_done")
        proj_ready = sem("proj_ready")
        rope_done = sem("rope_done")
        qh_done = sem("qh_done")
        ql_done = sem("ql_done")
        v_done = sem("v_done")
        vt_ready = sem("vt_ready")
        vv_done = sem("vv_done")
        k_stacked = sem("k_stacked")
        q_stacked = [sem(f"q_stacked{m}") for m in range(2)]
        max_ready = sem("max_ready")
        max_done = sem("max_done")
        mm_done = sem("mm_done")
        mt_ready = sem("mt_ready")
        mt_done = sem("mt_done")
        shift_in = [sem(f"shift_in{i}") for i in range(2)]
        score_ready = sem("score_ready")
        exp_done = sem("exp_done")
        causal_done = sem("causal_done")
        pv_done = sem("pv_done")
        norm = sem("norm")
        at_done = sem("at_done")
        ah_done = sem("ah_done")
        al_done = sem("al_done")
        out_ready = sem("out_ready")
        x1_done = sem("x1_done")
        x1_out = sem("x1_out")

        TILES = [(W_K, 2 * KV * D, 2), (W_KR, KV * D, 3), (W_Q, P, 4), (W_QR, P, 5),
                 (W_Q + P, P, 6), (W_QR + P, P, 7)]
        ROT = [(KV * D, 0, 1, 4, 5), (P, 2, 3, 0, 2), (P, 4, 5, 1, 3)]
        NR = len(ROT)

        block = ctx.enter_context(nc.Block())

        @block.sync
        def _(sp):
            sp.dma_start(pr_w, w0.rearrange("(k p) n -> p k n", p=P)).then_inc(w_in, 16)
            sp.dma_start(wb[:, :, :], w_bin.rearrange("(k p) n -> p k n", p=P)).then_inc(w_in, 16)
            sp.dma_start(bcol[:, :], bias_cols).then_inc(const, 16)
            for r in range(2):
                sp.dma_start(brow[:, r, :], bias_rows[r:r + 1, :].to_broadcast([P, E])).then_inc(const, 16)
            sp.dma_start(cos[:, :], rope[0]).then_inc(const, 16)
            sp.dma_start(sin[:, :], rope[1]).then_inc(const, 16)
            sp.wait_ge(fixed, 5)
            for half_ in range(2):
                for g in range(KV):
                    sp.dma_start(f32(ks[SHIFT + half_:SHIFT + half_ + 1, half_, g, :]), ones).then_inc(k_one, 16)
            sp.sem_inc(x1_out, 1)
            with sp.Fori(0, B) as b:
                sp.wait_ge(ql_done, b * (NR * NC) + NR + 1)
                for g in range(KV):
                    for half_ in range(2):
                        for piece, src in enumerate((kh, kh, kl)):
                            r = STACK * half_ + D * piece
                            sp.dma_start(f32(ks[r:r + D, half_, g, :]), f32(src[D * g:D * g + D, :])).then_inc(k_stacked, 16)
                for m in range(2):
                    sp.wait_ge(ql_done, b * (NR * NC) + NR + 2 + m)
                    for h in range(8 * m, 8 * m + 8):
                        for piece, src in enumerate((qh, ql, qh)):
                            r = STACK * (h % 2) + D * piece
                            sp.dma_start(f32(qs[r:r + D, h // 2, :]), f32(src[D * (h - 8 * m):D * (h - 8 * m) + D, m, :]))\
                              .then_inc(q_stacked[m], 16)
                for n, (c, g) in enumerate(ITEMS):
                    sp.wait_ge(mt_done, b * len(ITEMS) + n + 1)
                    for half_ in range(2):
                        sp.dma_start(f32(qs[SHIFT + half_:SHIFT + half_ + 1, 2 * g:2 * g + 2, c * CW:c * CW + CW]),
                                     f32(mt[2 * half_:2 * half_ + 2, n % 2, :])).then_inc(shift_in[n % 2], 16)
                for c in range(NC):
                    sp.wait_ge(x1_done, b * TT + TC * (c + 1) + 1)
                    sp.dma_start(x1[b, c * CW:c * CW + CW, :].rearrange("(t p) e -> p t e", p=P),
                                 xr[:, TC * c:TC * c + TC, :]).then_inc(x1_out, 16)
            sp.wait_ge(x1_out, B * NC * 16 + 1)

        @block.gpsimd
        def _(pool):
            def attention_lo(b, i):
                m, c = i % 2, i // 2
                pool.wait_ge(ah_done, b * 4 + i + 1)
                nc.gpsimd.tensor_tensor(ql[:, m, c * CW:c * CW + CW], at[:, i % 2, :],
                                        f32(qh[:, m, c * CW:c * CW + CW]), ALU.subtract).then_inc(al_done, 1)

            nc.gpsimd.memset(ident[:, :], 0.0).then_inc(fixed, 1)
            nc.gpsimd.memset(future[:, :], 0.0).then_inc(fixed, 1)
            nc.gpsimd.memset(half[:, :], -0.5).then_inc(fixed, 1)
            nc.gpsimd.memset(f32(ks[:, :, :, :]), 0.0).then_inc(fixed, 1)
            nc.gpsimd.memset(ones, 1.0).then_inc(fixed, 1)
            pool.wait_ge(fixed, 5)
            nc.gpsimd.affine_select(out=ident[:, :], in_=ident[:, :], compare_op=ALU.not_equal, fill=1.0,
                                    base=0, pattern=[[-1, P]], channel_multiplier=1).then_inc(fixed, 1)
            nc.gpsimd.affine_select(out=future[:, :], in_=future[:, :], compare_op=ALU.is_ge, fill=-1e30,
                                    base=0, pattern=[[-1, P]], channel_multiplier=1).then_inc(fixed, 1)
            nc.gpsimd.memset(vv[:, :, :, :], 1.0).then_inc(fixed, 1)
            pool.wait_ge(const, 5 * 16)
            nc.gpsimd.tensor_tensor(bsum[:, :], brow[:, 0, :], brow[:, 1, :], ALU.add).then_inc(fixed, 1)
            with pool.Fori(0, B) as b:
                pool.wait_ge(ln, b * 3 * TT + 1)
                pool.wait_ge(ln_pool, b * 3 + 1)
                pool.dma_start(xb[:, :, :], x[b].rearrange("(t p) e -> p t e", p=P)).then_inc(x_in, 16)
                wait_alone(pool, passed["pool"], ln, b * 3 * TT + 2 * TT + 1)
                nc.gpsimd.tensor_scalar(rstd[:, :], mv[:, :, 1], LN_EPS, None, ALU.add).then_inc(ln_pool, 1)
                pool.wait_ge(ln_pool, b * 3 + 2)
                nc.gpsimd.tensor_tensor(rstd[:, :], rstd[:, :], half[:, :], ALU.pow).then_inc(ln_pool, 1)
                pool.wait_ge(x1_out, b * NC * 16 + 1)
                nc.gpsimd.tensor_tensor(xr[:, :, :], xb[:, :, :], bsum[:, None, :].to_broadcast([P, TT, E]),
                                        ALU.add).then_inc(ln_pool, 1)
                for j in range(NR * NC):
                    c, r = j // NR, j % NR
                    rows = ROT[r][0]
                    cols = slice(c * CW, c * CW + CW)
                    lo, hi = (kl[:, cols], kh[:, cols]) if r == 0 else (ql[:, r - 1, cols], qh[:, r - 1, cols])
                    pool.wait_ge(qh_done, b * (NR * NC) + j + 1)
                    nc.gpsimd.tensor_tensor(lo, qf[0:rows, r, :], f32(hi), ALU.subtract).then_inc(ql_done, 1)
                k = 0
                for n in range(len(ITEMS)):
                    for kt, off, diagonal in key_tiles(n):
                        if diagonal:
                            wait_alone(pool, passed["pool"], exp_done, b * GROUPS_ALL * G + (k + 1) * G)
                            d = pr[:, k % P_SLOTS, :, off:off + P]
                            nc.gpsimd.affine_select(out=d, in_=d, compare_op=ALU.is_ge, fill=0.0, base=0,
                                                    pattern=[[0, G], [1, P]], channel_multiplier=-1)\
                              .then_inc(causal_done, 1)
                        k += 1
                    if n >= 2 and n % 2 == 0:
                        attention_lo(b, n // 2 - 1)
                attention_lo(b, len(ITEMS) // 2 - 1)

        @block.scalar
        def _(act):
            def attention_hi(act, b, i):
                m, c = i % 2, i // 2
                act.wait_ge(at_done, b * 4 + i + 1)
                nc.scalar.activation(qh[:, m, c * CW:c * CW + CW], at[:, i % 2, :], ACT.Copy).then_inc(ah_done, 1)

            act.wait_ge(w_in, 32)
            for k in range(KE):
                nc.scalar.activation(wabs_out[:, k, :], wb[:, k, :], ACT.Abs, accum_out=wabs[:, k, :]).then_inc(w_abs, 1)
            nc.scalar.activation(wh[:, :, 0:W_ALL0], pr_w, ACT.Copy).then_inc(w_hi, 1)
            act.wait_ge(fixed, 7)
            nc.scalar.activation(identb[:, :], ident[:, :], ACT.Copy).then_inc(w_hi, 1)
            for k in range(KE):
                act.wait_ge(w_bt, k + 1)
                nc.scalar.activation(wh[:, k, W_BIN:W_ALL], ps[:, k, 0:E], ACT.Copy).then_inc(w_hi, 1)
            with act.Fori(0, B) as b:
                for j in range(NC * KE):
                    c, k = j // KE, j % KE
                    act.wait_ge(xt_ready, b * (NC * KE) + j + 1)
                    nc.scalar.activation(xh[:, k, c * CW:c * CW + CW], ps[:, k, :], ACT.Copy).then_inc(xh_done, 1)
                    if k < KE - 1:
                        continue
                    cols = slice(c * CW, c * CW + CW)
                    act.wait_ge(proj_ready, b * (NC * 6) + 6 * c + 1)
                    nc.scalar.activation(vt[64:128, cols], ps[64:128, 2, :], ACT.Identity,
                                         bias=bcol[64:128, 4:5]).then_inc(v_done, 1)
                    for r, (rows, *_) in enumerate(ROT):
                        hi = kh[:, cols] if r == 0 else qh[:, r - 1, cols]
                        act.wait_ge(rope_done, b * (3 * NR * NC) + 3 * NR * c + 3 * r + 3)
                        nc.scalar.activation(hi, qf[0:rows, r, :], ACT.Copy).then_inc(qh_done, 1)

                def shift_row(n):
                    act.wait_ge(mt_ready, b * len(ITEMS) + n + 1)
                    nc.scalar.activation(mt[:, n % 2, :], ps[0:G, BANK_X, :], ACT.Copy, scale=-1.0).then_inc(mt_done, 1)

                shift_row(0)
                k = 0
                for n in range(len(ITEMS)):
                    for j, (kt, off, diagonal) in enumerate(key_tiles(n)):
                        if k >= P_SLOTS:
                            act.wait_ge(pv_done, b * GROUPS_ALL + k - P_SLOTS + 1)
                        for i in range(G):
                            u = G * k + i
                            act.wait_ge(score_ready, b * GROUPS_ALL * G + u + 1)
                            nc.scalar.activation(pr[:, k % P_SLOTS, i, off:CW], ps[:, BANK_S + u % 2, off:CW],
                                                 ACT.Exp, scale=float(D) ** -0.5).then_inc(exp_done, 1)
                        if j == 1 and n + 1 < len(ITEMS):
                            shift_row(n + 1)
                        k += 1
                        if j == 2 and n >= 2 and n % 2 == 0:
                            attention_hi(act, b, n // 2 - 1)
                attention_hi(act, b, 3)

        @block.tensor
        def _(pe):
            def three(out, lh, ll, rh, rl, start, stop):
                nc.tensor.matmul(out, lh, rh, start=start, stop=False)
                nc.tensor.matmul(out, ll, rh, start=False, stop=False)
                return nc.tensor.matmul(out, lh, rl, start=False, stop=stop)

            pe.wait_ge(fixed, 7)
            pe.wait_ge(w_bw, 7)
            for k in range(KE):
                for o in range(KE):
                    mm_ = nc.tensor.transpose(ps[:, k, o * P:o * P + P], wt[:, o, k * P:k * P + P], ident[:, :])
                mm_.then_inc(w_bt, 1)
            pe.wait_ge(w_hi, 2 + KE)
            pe.wait_ge(w_lo, 1 + KE)
            pe.wait_ge(k_one, 2 * KV * 16)
            pe.wait_ge(fixed, 9)
            with pe.Fori(0, B) as b:
                pe.wait_ge(x1_done, b * TT + 1)
                pe.wait_ge(ln, b * 3 * TT + 3 * TT + 1)
                for c in range(NC):
                    if c:
                        pe.wait_ge(xl_done, b * (NC * KE) + c * KE)
                    for k in range(KE):
                        for t in range(TC):
                            mm_ = nc.tensor.transpose(ps[:, k, t * P:t * P + P],
                                                      xn[:, TC * c + t, k * P:k * P + P], ident[:, :])
                        mm_.then_inc(xt_ready, 1)
                    pe.wait_ge(xl_done, b * (NC * KE) + (c + 1) * KE)
                    for j, (w, cols, bank) in enumerate(TILES):
                        if c:
                            pe.wait_ge(rope_done, b * (3 * NR * NC) + 3 * (j // 2) + 1 + j % 2)
                            if j == 0:
                                pe.wait_ge(v_done, b * NC + c)
                        for k in range(KE):
                            r = slice(c * CW, c * CW + CW)
                            mm_ = three(ps[0:cols, bank, :], wh[:, k, w:w + cols], wl[:, k, w:w + cols],
                                        xh[:, k, r], xl[:, k, r], k == 0, k == KE - 1)
                        mm_.then_inc(proj_ready, 1)
                wait_alone(pe, passed["pe"], v_done, b * NC + NC)
                for t in range(TT):
                    mm_ = nc.tensor.transpose(ps[:, 0, t * 64:t * 64 + 64], vt[64:128, t * P:t * P + P],
                                              ident[64:128, 64:128])
                mm_.then_inc(vt_ready, 1)
                pe.wait_ge(rope_done, (b + 1) * (3 * NR * NC))
                pe.wait_ge(vv_done, b + 1)
                pe.wait_ge(k_stacked, (b + 1) * (KV * 2 * PIECES * 16))
                pe.wait_ge(q_stacked[0], (b + 1) * (8 * PIECES * 16))

                unit = 0

                def max_unit(n, qt, pair, k0, width):
                    nonlocal unit
                    g = ITEMS[n][1]
                    if unit >= 2:
                        pe.wait_ge(max_done, b * UNITS_ALL + unit - 1)
                    diagonal = k0 + width == (qt + 1) * P
                    for half_ in range(2):
                        bank = ps[:, 2 * (unit % 2) + half_, :]
                        mm_ = nc.tensor.matmul(bank[:, 0:width], qs[0:PAIR, 2 * g + pair, qt * P:qt * P + P],
                                               ks[0:PAIR, half_, g, k0:k0 + width], start=True, stop=not diagonal)
                        if diagonal:
                            mm_ = nc.tensor.matmul(bank[:, width - P:width], identb[:, :], future[:, :],
                                                   start=False, stop=True)
                    mm_.then_inc(max_ready, 1)
                    unit += 1

                def max_rows(n):
                    pe.wait_ge(mm_done, b * len(ITEMS) + n + 1)
                    if n:
                        pe.wait_ge(mt_done, b * len(ITEMS) + n)
                    for t in range(TC):
                        mm_ = nc.tensor.transpose(ps[0:G, BANK_X, t * P:t * P + P], mm[:, n % 2, t, :], ident[:, :])
                    mm_.then_inc(mt_ready, 1)

                def weigh(k):
                    n, j = GROUP_OF[k]
                    c, g = ITEMS[n]
                    kt, off, diagonal = key_tiles(n)[j]
                    if j == 0 and n:
                        pe.wait_ge(norm, (b * len(ITEMS) + n - 1) * NORM + 1)
                    if diagonal:
                        pe.wait_ge(causal_done, b * DIAG_ALL + int(DIAGONALS[k]))
                    else:
                        pe.wait_ge(exp_done, b * GROUPS_ALL * G + (k + 1) * G)
                    for i in range(G):
                        mm_ = nc.tensor.matmul(ps[32 * i:32 * i + 32, BANK_O, off:CW], vv[:, kt, g, :],
                                               pr[:, k % P_SLOTS, i, off:CW],
                                               start=(j == 0), stop=(j == GROUPS[n] - 1))
                    mm_.then_inc(pv_done, 1)

                for n in range(LOOKAHEAD):
                    for u in max_units(n):
                        max_unit(n, *u)
                max_rows(0)
                k = 0
                for n, (c, g) in enumerate(ITEMS):
                    if n == 0:
                        pe.wait_ge(q_stacked[1], (b + 1) * (8 * PIECES * 16))
                    ahead = [(n + LOOKAHEAD, u) for u in max_units(n + LOOKAHEAD)] if n + LOOKAHEAD < len(ITEMS) else []
                    pe.wait_ge(shift_in[n % 2], b * (len(ITEMS) // 2 * 32) + (n // 2 + 1) * 32)
                    tiles = key_tiles(n)
                    issued = 0
                    for j, (kt, off, diagonal) in enumerate(tiles):
                        for i in range(G):
                            u = G * k + i
                            if u >= 2:
                                pe.wait_ge(exp_done, b * GROUPS_ALL * G + u - 1)
                            nc.tensor.matmul(ps[:, BANK_S + u % 2, off:CW], ks[0:ROWS, i % 2, g, kt * P:kt * P + P],
                                             qs[0:ROWS, 2 * g + i // 2, c * CW + off:c * CW + CW],
                                             start=True, stop=True).then_inc(score_ready, 1)
                            want = (len(ahead) * (G * j + i + 1)) // (G * len(tiles))
                            while issued < want:
                                max_unit(ahead[issued][0], *ahead[issued][1])
                                issued += 1
                            if i == 1 and k:
                                weigh(k - 1)
                        if j == 0 and n + 1 < len(ITEMS):
                            max_rows(n + 1)
                        k += 1
                weigh(GROUPS_ALL - 1)

                for t in range(TT):
                    if t % TC == 0:
                        pe.wait_ge(al_done, b * 4 + 2 * (t // TC) + 2)
                    if t >= TC:
                        pe.wait_ge(x1_done, b * TT + t - TC + 2)
                    elif t == 0:
                        pe.wait_ge(max_done, (b + 1) * UNITS_ALL)
                    r = slice(t * P, t * P + P)
                    bank = ps[:, t % TC, 0:E]
                    for k in range(KE):
                        three(bank, qh[:, k, r], ql[:, k, r], wh[:, k, W_O:W_O + E], wl[:, k, W_O:W_O + E], k == 0, False)
                    for k in range(KE):
                        mm_ = three(bank, xh[:, k, r], xl[:, k, r], wh[:, k, W_BIN:W_ALL], wl[:, k, W_BIN:W_ALL],
                                    False, k == KE - 1)
                    mm_.then_inc(out_ready, 1)

        @block.vector
        def _(dve):
            dve.wait_ge(w_in, 32)
            for k in range(KE):
                nc.vector.tensor_scalar(wt[:, k, :], wb[:, k, :], 0.0, 2.0, ALU.is_ge, ALU.mult).then_inc(w_bw, 1)
            dve.wait_ge(w_abs, KE)
            nc.vector.tensor_scalar(wabs[:, :, :], wabs[:, :, :], 1.0 / E, None, ALU.mult).then_inc(w_bw, 1)
            dve.wait_ge(w_bw, KE + 1)
            for k in range(KE):
                nc.vector.tensor_scalar(wt[:, k, :], wt[:, k, :], -1.0, wabs[:, k, :], ALU.add, ALU.mult).then_inc(w_bw, 1)
            dve.wait_ge(w_bw, 2 * KE + 1)
            nc.vector.tensor_tensor(wt[:, :, :], wt[:, :, :], wb[:, :, :], ALU.subtract).then_inc(w_bw, 1)
            dve.wait_ge(w_bw, 2 * KE + 2)
            nc.vector.tensor_tensor(wt[:, :, :], wt[:, :, :], wb[:, :, :], ALU.add).then_inc(w_bw, 1)
            dve.wait_ge(w_hi, 1)
            nc.vector.tensor_tensor(wl[:, :, 0:W_ALL0], pr_w, f32(wh[:, :, 0:W_ALL0]), ALU.subtract).then_inc(w_lo, 1)
            for k in range(KE):
                dve.wait_ge(w_hi, 3 + k)
                nc.vector.tensor_tensor(wl[:, k, W_BIN:W_ALL], ps[:, k, 0:E], f32(wh[:, k, W_BIN:W_ALL]), ALU.subtract)\
                  .then_inc(w_lo, 1)
            dve.wait_ge(w_lo, 1 + KE)
            dve.wait_ge(const, 5 * 16)
            dve.sem_inc(x1_done, 1)
            dve.sem_inc(ln, 1)
            dve.sem_inc(ln_pool, 1)
            dve.wait_ge(fixed, 9)
            dve.wait_ge(k_one, 2 * KV * 16)
            with dve.Fori(0, B) as b:
                dve.wait_ge(x_in, b * 16 + 16)
                for t in range(TT):
                    nc.vector.bn_stats(stats[:, t, :], xb[:, t, :]).then_inc(ln, 1)
                wait_alone(dve, passed["dve"], ln, b * 3 * TT + TT + 1)
                for t in range(TT):
                    nc.vector.bn_aggr(mv[:, t, :], stats[:, t, :]).then_inc(ln, 1)
                dve.wait_ge(ln_pool, b * 3 + 3)
                dve.wait_ge(ln, b * 3 * TT + 2 * TT + 1)
                for t in range(TT):
                    nc.vector.tensor_scalar(xn[:, t, :], xb[:, t, :], mv[:, t, 0:1], rstd[:, t:t + 1],
                                            ALU.subtract, ALU.mult).then_inc(ln, 1)
                for c in range(NC):
                    cols = slice(c * CW, c * CW + CW)
                    for k in range(KE):
                        dve.wait_ge(xh_done, b * (NC * KE) + c * KE + k + 1)
                        nc.vector.tensor_tensor(xl[:, k, cols], ps[:, k, :], f32(xh[:, k, cols]), ALU.subtract)\
                          .then_inc(xl_done, 1)
                    for r, (rows, j0, j1, b0, b1) in enumerate(ROT):
                        before = b * (3 * NR * NC) + 3 * NR * c + 3 * r
                        dve.wait_ge(proj_ready, b * (NC * 6) + 6 * c + j0 + 1)
                        if c or r:
                            dve.wait_ge(rope_done, before)
                        nc.vector.scalar_tensor_tensor(t1[0:rows], ps[0:rows, 2 + j0, :], bcol[0:rows, b0:b0 + 1],
                                                       cos[0:rows, cols], ALU.add, ALU.mult).then_inc(rope_done, 1)
                        dve.wait_ge(proj_ready, b * (NC * 6) + 6 * c + j1 + 1)
                        nc.vector.scalar_tensor_tensor(t2[0:rows], ps[0:rows, 2 + j1, :], bcol[0:rows, b1:b1 + 1],
                                                       sin[0:rows, cols], ALU.add, ALU.mult).then_inc(rope_done, 1)
                        dve.wait_ge(rope_done, before + 2)
                        if c:
                            dve.wait_ge(ql_done, b * (NR * NC) + NR * (c - 1) + r + 1)
                        nc.vector.tensor_tensor(qf[0:rows, r, :], t1[0:rows], t2[0:rows], ALU.add).then_inc(rope_done, 1)
                dve.wait_ge(vt_ready, b + 1)
                nc.vector.tensor_copy(vv[:, :, :, 0:D].rearrange("p t g d -> p (t g) d"),
                                      ps[:, 0, :].rearrange("p (t d) -> p t d", d=D)).then_inc(vv_done, 1)

                def normalise(n):
                    c, g = ITEMS[n]
                    base = (b * len(ITEMS) + n) * NORM
                    o = ot[:, g % 2, :].rearrange("p (k r) -> p k r", r=2 * D)
                    dve.wait_ge(pv_done, b * GROUPS_ALL + sum(GROUPS[:n + 1]))
                    if n:
                        dve.wait_ge(norm, base)
                    nc.vector.transpose(ot[:, g % 2, :], ps[:, BANK_O, :]).then_inc(norm, 1)
                    dve.wait_ge(norm, base + 1)
                    nc.vector.reciprocal(rc[:, g % 2, :], o[:, :, D]).then_inc(norm, 1)
                    dve.wait_ge(norm, base + 2)
                    if n >= 2:
                        dve.wait_ge(at_done, b * 4 + n // 2)
                    nc.vector.tensor_tensor(nm[:, :].rearrange("p (k r) -> p k r", r=2 * D)[:, :, D * (g % 2):D * (g % 2) + D],
                                            o[:, :, 0:D],
                                            rc[:, g % 2, :, None].to_broadcast([P, CW // (2 * D), D]), ALU.mult)\
                      .then_inc(norm, 1)
                    if g % 2:
                        dve.wait_ge(norm, base + 3)
                        if n >= 4:
                            dve.wait_ge(al_done, b * 4 + n // 2 - 1)
                        nc.vector.transpose(at[:, (n // 2) % 2, :], nm[:, :]).then_inc(at_done, 1)

                unit = 0
                for n in range(len(ITEMS) + 2):
                    if n >= len(ITEMS):
                        normalise(n - 3)
                        continue
                    if n >= 2:
                        dve.wait_ge(mt_ready, b * len(ITEMS) + n - 1)
                    c = ITEMS[n][0]
                    for j, (qt, pair, k0, width) in enumerate(max_units(n)):
                        dve.wait_ge(max_ready, b * UNITS_ALL + unit + 1)
                        dst = mx[:, n % 2, k0 // CW, qt % TC, pair::2] if c else mm[:, n % 2, qt % TC, pair::2]
                        src = ps[:, 2 * (unit % 2):2 * (unit % 2) + 2, 0:width]
                        nc.vector.tensor_reduce(dst, src, AX_X, ALU.max).then_inc(max_done, 1)
                        unit += 1
                        if j == 2 and n >= 3:
                            normalise(n - 3)
                    if c:
                        dve.wait_ge(max_done, b * UNITS_ALL + unit)
                        nc.vector.tensor_tensor(mm[:, n % 2, :, :], mx[:, n % 2, 0, :, :], mx[:, n % 2, 1, :, :], ALU.max)\
                          .then_inc(mm_done, 1)
                    else:
                        dve.wait_ge(max_done, b * UNITS_ALL + unit)
                        dve.sem_inc(mm_done, 1)
                normalise(len(ITEMS) - 1)
                for t in range(TT):
                    dve.wait_ge(out_ready, b * TT + t + 1)
                    if t == 0:
                        dve.wait_ge(ln_pool, b * 3 + 4)
                    nc.vector.tensor_tensor(xr[:, t, :], ps[:, t % TC, 0:E], xr[:, t, :], ALU.add).then_inc(x1_done, 1)

CHUNKS = B * NC
DFF, MLP = 1024, 2048
MU, MF = DFF // P, MLP // P
RMS_EPS = 1.1920929e-07
CUM_EPS = 1e-6
BLOCK_ROWS = 32 // 2
GU_SLICES = 2 * MLP // CW
DN_SLICES = MF // 2 * E // CW
NIBBLES = 2
DQ_DVE = 7


def steps(engine, front, back, both):
    front(0, 0)
    with engine.Fori(0, B - 1) as b:
        both(2 * b + 1, 1)
        both(2 * b + 2, 0)
    both(CHUNKS - 1, 1)
    back(CHUNKS - 1, 1)


def later(ch):
    return not isinstance(ch, int) or ch > 0


def load_codes(sp, packed, scales, codes, scale_rows, sem):
    sp.dma_start(codes, packed).then_inc(sem, 16)
    for a in range(P // BLOCK_ROWS):
        sp.dma_start(scale_rows[a * BLOCK_ROWS:(a + 1) * BLOCK_ROWS], scales[a:a + 1].to_broadcast([BLOCK_ROWS, CW]))\
          .then_inc(sem, 16)


LOADS = 16 * (1 + P // BLOCK_ROWS)


def dequantize(nc, dve, codes, scale_rows, bits, mag, out, done, before):
    for e in range(NIBBLES):
        at = before + e * DQ_DVE
        m, b = mag[:, e, :], bits[:, e, :]
        nc.vector.tensor_scalar(b, codes, 4 * e, 7, ALU.logical_shift_right, ALU.bitwise_and).then_inc(done, 1)
        dve.wait_ge(done, at + 1)
        nc.vector.tensor_scalar(m.bitcast(I32), b, float(1 << 22), float(126 << 23), ALU.mult, ALU.add).then_inc(done, 1)
        dve.wait_ge(done, at + 2)
        nc.vector.tensor_scalar(b.bitcast(F32), m, 2.0, -1.0, ALU.mult, ALU.add).then_inc(done, 1)
        dve.wait_ge(done, at + 3)
        nc.vector.tensor_tensor(m, m, b.bitcast(F32), ALU.min).then_inc(done, 1)
        dve.wait_ge(done, at + 4)
        nc.vector.tensor_scalar(b, codes, 28 - 4 * e, -(1 << 31), ALU.logical_shift_left, ALU.bitwise_and).then_inc(done, 1)
        nc.vector.tensor_tensor(m, m, scale_rows, ALU.mult).then_inc(done, 1)
        dve.wait_ge(done, at + 6)
        nc.vector.tensor_tensor(out[:, e, :].bitcast(I32), m.bitcast(I32), b, ALU.bitwise_or).then_inc(done, 1)



def phase_b1(nc, x1, w_qkv, w_swiglu, w_out, gu_codes, gu_scales, guh, gul, att):
    with ExitStack() as ctx:
        def sb(name, shape, dt=F32):
            return ctx.enter_context(nc.sbuf_tensor("b_" + name, shape, dt))

        def sem(name):
            return ctx.enter_context(nc.semaphore("b_" + name))

        W_COLS = [3 * E, 2 * DFF, MU * E // KE]
        qkvh, qkvl = sb("qkvh", [P, KE, 3 * E], F32R), sb("qkvl", [P, KE, 3 * E], F32R)
        swh, swl = sb("swh", [P, KE, 2 * DFF], F32R), sb("swl", [P, KE, 2 * DFF], F32R)
        woh, wol = sb("woh", [P, MU, E], F32R), sb("wol", [P, MU, E], F32R)
        xh, xl = sb("xh", [P, KE, CW], F32R), sb("xl", [P, KE, CW], F32R)
        yh, yl = sb("yh", [P, KE, CW], F32R), sb("yl", [P, KE, CW], F32R)
        F_RING = 4
        fh, fl = sb("fh", [P, F_RING, CW], F32R), sb("fl", [P, F_RING, CW], F32R)
        arena = sb("arena", [P, 22 * CW])

        def part(first, n):
            return arena[:, first * CW:(first + n) * CW].rearrange("p (a t) -> p a t", t=CW)

        xb = part(0, 2).rearrange("p a t -> p (a t)").rearrange("p (t e) -> p t e", e=E)
        kk, qq, vv = part(2, 2), part(4, 2), part(6, 2)
        wc, kc = part(8, 2), part(10, 2)
        sqk, sqq = wc, kc
        rk, rq = part(12, 1), part(13, 1)
        sg = part(14, 2)
        ao = part(16, 2)
        bits, mag = part(18, 2).bitcast(I32), part(20, 2)
        codes = sb("codes", [P, CW], I32)
        scale_rows = sb("scale_rows", [P, CW])
        ones = sb("ones", [P, CW])
        mean = sb("mean", [P, P])
        ident = sb("ident", [P, P])
        stats = sb("stats", [P, TC, 6])
        mv = sb("mv", [P, TC, 2])
        s1, s2, half = sb("s1", [P, TC]), sb("s2", [P, TC]), sb("half", [P, TC])
        eps = sb("eps", [P, 1])
        carry = sb("carry", [P, 2, KE])
        raw_qkv = arena[:, 0:KE * 3 * E].rearrange("p (k n) -> p k n", k=KE)
        o1 = KE * 3 * E
        raw_sw = arena[:, o1:o1 + KE * 2 * DFF].rearrange("p (k n) -> p k n", k=KE)
        o2 = o1 + KE * 2 * DFF
        raw_wo = arena[:, o2:o2 + MU * E].rearrange("p (k n) -> p k n", k=MU)
        assert o2 + MU * E <= 22 * CW
        ps = ctx.enter_context(nc.psum_tensor("b_ps", [P, 8, CW], F32))
        BANK_UG, BANK_OUT = 2, 6

        passed = {e: sem("passed_" + e) for e in ("dve", "pool")}
        w_in = [sem(f"w_in{i}") for i in range(3)]
        w_hi, w_lo = sem("w_hi"), sem("w_lo")
        fixed = sem("fixed")
        x_in = sem("x_in")
        ln, ln_pool = sem("ln"), sem("ln_pool")
        xt_ready, xh_done, xl_done = sem("xt_ready"), sem("xh_done"), sem("xl_done")
        qkv_ready = sem("qkv_ready")
        kq_copied, squared, v_copied = sem("kq_copied"), sem("squared"), sem("v_copied")
        ms_ready = sem("ms_ready")
        rms_ln, rms_done = sem("rms_ln"), sem("rms_done")
        scaled = sem("scaled")
        exp_done = sem("exp_done")
        wv_done, scan_done, carried = sem("wv_done"), sem("scan_done"), sem("carried")
        plus_one = sem("plus_one")
        quotient = sem("quotient")
        yh_done, yl_done = sem("yh_done"), sem("yl_done")
        ug_ready, silu_done, f_done = sem("ug_ready"), sem("silu_done"), sem("f_done")
        fh_done, fl_done = sem("fh_done"), sem("fl_done")
        summed = sem("summed")
        ao_done, ao_out = sem("ao_done"), sem("ao_out")
        codes_in, dq, gh_done, gl_done = sem("codes_in"), sem("dq"), sem("gh_done"), sem("gl_done")

        block = ctx.enter_context(nc.Block())

        @block.sync
        def _(sp):
            for i, (raw, w) in enumerate(((raw_qkv, w_qkv), (raw_sw, w_swiglu), (raw_wo, w_out))):
                sp.dma_start(raw, w.rearrange("(k p) n -> p k n", p=P)).then_inc(w_in[i], 16)

            def front(ch, odd):
                sp.wait_ge(xt_ready, ch * KE + 1)
                sp.dma_start(xb, x1[ch].rearrange("(t p) e -> p t e", p=P)).then_inc(x_in, 16)
                sp.wait_ge(dq, ch * (NIBBLES * DQ_DVE) + 1)
                load_codes(sp, gu_codes[ch], gu_scales[ch], codes[:, :], scale_rows, codes_in)

            def back(ch, odd):
                sp.wait_ge(ao_done, ch + 2)
                sp.dma_start(att[ch], ao).then_inc(ao_out, 16)

            def both(ch, odd):
                front(ch, odd)
                back(ch - 1, 1 - odd)

            sp.wait_ge(w_hi, 3)
            sp.wait_ge(w_lo, 3)
            sp.sem_inc(ao_out, 1)
            steps(sp, front, back, both)
            sp.wait_ge(ao_out, CHUNKS * 16 + 1)

        @block.gpsimd
        def _(pool):
            nc.gpsimd.memset(ident[:, :], 0.0).then_inc(fixed, 1)
            nc.gpsimd.memset(half[:, :], -0.5).then_inc(fixed, 1)
            nc.gpsimd.memset(ones[:, :], 1.0).then_inc(fixed, 1)
            nc.gpsimd.memset(mean[:, :], 1.0 / E).then_inc(fixed, 1)
            nc.gpsimd.memset(eps[:, :], RMS_EPS).then_inc(fixed, 1)
            pool.wait_ge(fixed, 5)
            nc.gpsimd.affine_select(out=ident[:, :], in_=ident[:, :], compare_op=ALU.not_equal, fill=1.0,
                                    base=0, pattern=[[-1, P]], channel_multiplier=1).then_inc(fixed, 1)

            def norm_scales(ch):
                var = mv[:, :, 1]
                chain = [lambda: nc.gpsimd.tensor_scalar(s1[:, :], var, LN_EPS, None, ALU.add),
                         lambda: nc.gpsimd.tensor_tensor(s1[:, :], s1[:, :], half[:, :], ALU.pow),
                         lambda: nc.gpsimd.tensor_tensor(s2[:, :], s1[:, :], s1[:, :], ALU.mult),
                         lambda: nc.gpsimd.tensor_tensor(s2[:, :], s2[:, :], var, ALU.mult),
                         lambda: nc.gpsimd.tensor_scalar(s2[:, :], s2[:, :], RMS_EPS, None, ALU.add),
                         lambda: nc.gpsimd.tensor_tensor(s2[:, :], s2[:, :], half[:, :], ALU.pow),
                         lambda: nc.gpsimd.tensor_tensor(s2[:, :], s2[:, :], s1[:, :], ALU.mult)]
                wait_alone(pool, passed["pool"], ln, ch * (3 * TC) + 2 * TC)
                for i, step in enumerate(chain):
                    if i:
                        wait_alone(pool, passed["pool"], ln_pool, ch * 7 + i)
                    step().then_inc(ln_pool, 1)

            def e_plus_one(ch):
                wait_alone(pool, passed["pool"], exp_done, ch * 2 + 2)
                nc.gpsimd.tensor_scalar(qq, qq, 1.0, None, ALU.add).then_inc(plus_one, 1)

            def y_lo(ch):
                pool.wait_ge(yh_done, ch + 1)
                nc.gpsimd.tensor_tensor(yl[:, :, :], qq, f32(yh[:, :, :]), ALU.subtract).then_inc(yl_done, 1)

            def gate_lo(ch):
                pool.wait_ge(gh_done, ch + 1)
                nc.gpsimd.tensor_tensor(gul[:, ch, :, :], mag, f32(guh[:, ch, :, :]), ALU.subtract).then_inc(gl_done, 1)

            def f_lo(ch, j):
                pool.wait_ge(fh_done, ch * MU + j + 1)
                nc.gpsimd.tensor_tensor(fl[:, j % F_RING, :], sg[:, j % 2, :], f32(fh[:, j % F_RING, :]), ALU.subtract)\
                  .then_inc(fl_done, 1)

            def front(ch, odd):
                norm_scales(ch)
                e_plus_one(ch)
                y_lo(ch)
                gate_lo(ch)

            def back(ch, odd):
                for j in range(MU):
                    f_lo(ch, j)

            def both(ch, odd):
                norm_scales(ch)
                for j in range(4):
                    f_lo(ch - 1, j)
                e_plus_one(ch)
                for j in range(4, MU):
                    f_lo(ch - 1, j)
                y_lo(ch)
                gate_lo(ch)

            steps(pool, front, back, both)

        @block.scalar
        def _(act):
            for i, (hi, raw) in enumerate(((qkvh, raw_qkv), (swh, raw_sw), (woh, raw_wo))):
                act.wait_ge(w_in[i], 16)
                nc.scalar.activation(hi[:, :, :], raw, ACT.Copy).then_inc(w_hi, 1)

            def project(ch):
                for k in range(KE):
                    act.wait_ge(xt_ready, ch * KE + k + 2)
                    nc.scalar.activation(xh[:, k, :], ps[:, k, :], ACT.Copy).then_inc(xh_done, 1)
                for j in range(2 * KE):
                    dst, sq = (kk, sqk) if j < KE else (qq, sqq)
                    act.wait_ge(qkv_ready, ch * (3 * KE) + j + 1)
                    nc.scalar.activation(dst[:, j % KE, :], ps[:, j % 2, :], ACT.Copy).then_inc(kq_copied, 1)
                    nc.scalar.activation(sq[:, j % KE, :], ps[:, j % 2, :], ACT.Square).then_inc(squared, 1)

            def exponentials(ch):
                for i, r in enumerate((rk, rq)):
                    act.wait_ge(ms_ready, ch * 2 + i + 1)
                    nc.scalar.activation(r, ps[:, i:i + 1, :], ACT.Ln, bias=eps[:, :]).then_inc(rms_ln, 1)
                    act.wait_ge(rms_ln, ch * 2 + i + 1)
                    nc.scalar.activation(r, r, ACT.Exp, scale=-0.5).then_inc(rms_done, 1)
                for i, (t, scale) in enumerate(((kk, 1.0), (qq, -1.0))):
                    act.wait_ge(scaled, ch * 2 + i + 1)
                    nc.scalar.activation(t, t, ACT.Exp, scale=scale).then_inc(exp_done, 1)

            def gate_hi(ch):
                act.wait_ge(dq, (ch + 1) * (NIBBLES * DQ_DVE) + 1)
                nc.scalar.activation(guh[:, ch, :, :], mag, ACT.Copy).then_inc(gh_done, 1)

            def y_hi(ch):
                act.wait_ge(quotient, ch * 3 + 3)
                nc.scalar.activation(yh[:, :, :], qq, ACT.Copy).then_inc(yh_done, 1)

            def silu(ch, j):
                act.wait_ge(ug_ready, ch * MU + j + 1)
                if j >= 2:
                    act.wait_ge(fl_done, ch * MU + j - 1)
                nc.scalar.activation(sg[:, j % 2, :], ps[:, BANK_UG + 2 * (j % 2) + 1, :], ACT.Silu).then_inc(silu_done, 1)

            def f_hi(ch, j):
                act.wait_ge(f_done, ch * MU + j + 3)
                if j >= F_RING:
                    act.wait_ge(summed, ch * MU + j - F_RING + 1)
                nc.scalar.activation(fh[:, j % F_RING, :], sg[:, j % 2, :], ACT.Copy).then_inc(fh_done, 1)

            def half_back(ch, js):
                js = list(js)
                silu(ch, js[0])
                for j in js[1:]:
                    silu(ch, j)
                    f_hi(ch, j - 1)
                f_hi(ch, js[-1])

            def sums_out(ch):
                act.wait_ge(summed, (ch + 1) * MU)
                act.wait_ge(ao_out, ch * 16 + 1)
                nc.scalar.activation(ao, ps[:, BANK_OUT:BANK_OUT + KE, :], ACT.Copy).then_inc(ao_done, 1)

            def front(ch, odd):
                project(ch)
                exponentials(ch)
                y_hi(ch)
                gate_hi(ch)

            def back(ch, odd):
                half_back(ch, range(4))
                half_back(ch, range(4, MU))
                sums_out(ch)

            def both(ch, odd):
                half_back(ch - 1, range(4))
                project(ch)
                exponentials(ch)
                half_back(ch - 1, range(4, MU))
                y_hi(ch)
                gate_hi(ch)
                sums_out(ch - 1)

            steps(act, front, back, both)

        @block.tensor
        def _(pe):
            def three(out, lh, ll, rh, rl, start, stop):
                nc.tensor.matmul(out, lh, rh, start=start, stop=False)
                nc.tensor.matmul(out, ll, rh, start=False, stop=False)
                return nc.tensor.matmul(out, lh, rl, start=False, stop=stop)

            def project(ch):
                pe.wait_ge(ln, (ch + 1) * (3 * TC))
                for k in range(KE):
                    if later(ch):
                        pe.wait_ge(rms_ln, ch * 2 + k - 1)
                    for t in range(TC):
                        mm = nc.tensor.transpose(ps[:, k, t * P:t * P + P], xb[:, t, k * P:k * P + P], ident[:, :])
                    mm.then_inc(xt_ready, 1)
                pe.wait_ge(xl_done, ch * KE + KE)
                for j, w in enumerate((E, E + P, 0, P, 2 * E, 2 * E + P)):
                    if 2 <= j:
                        pe.wait_ge(squared, ch * (2 * KE) + j - 1)
                    for k in range(KE):
                        mm = three(ps[:, j % 2, :], qkvh[:, k, w:w + P], qkvl[:, k, w:w + P],
                                   xh[:, k, :], xl[:, k, :], k == 0, k == KE - 1)
                    mm.then_inc(qkv_ready, 1)

            def mean_squares(ch):
                for i, sq in enumerate((sqk, sqq)):
                    pe.wait_ge(v_copied, ch * KE + i + 1)
                    pe.wait_ge(squared, ch * (2 * KE) + 2 * i + 2)
                    for k in range(KE):
                        mm = nc.tensor.matmul(ps[:, i, :], mean[:, :], sq[:, k, :], start=k == 0, stop=k == KE - 1)
                    mm.then_inc(ms_ready, 1)

            def up_gate(ch, j):
                if j == 0:
                    pe.wait_ge(yl_done, ch + 1)
                pe.wait_ge(f_done, ch * MU + j + 1)
                for i in range(2):
                    w = i * DFF + j * P
                    for k in range(KE):
                        mm = three(ps[:, BANK_UG + 2 * (j % 2) + i, :], swh[:, k, w:w + P], swl[:, k, w:w + P],
                                   yh[:, k, :], yl[:, k, :], k == 0, k == KE - 1)
                mm.then_inc(ug_ready, 1)

            def sum_out(ch, j):
                pe.wait_ge(fl_done, ch * MU + j + 1)
                if j == 0:
                    pe.wait_ge(ao_done, ch + 1)
                for i in range(KE):
                    mm = three(ps[:, BANK_OUT + i, :], woh[:, j, i * P:i * P + P], wol[:, j, i * P:i * P + P],
                               fh[:, j % F_RING, :], fl[:, j % F_RING, :], j == 0, j == MU - 1)
                mm.then_inc(summed, 1)

            def front(ch, odd):
                project(ch)
                mean_squares(ch)

            def back(ch, odd):
                for j in range(4):
                    up_gate(ch, j)
                for j in range(4):
                    sum_out(ch, j)
                for j in range(4, MU):
                    up_gate(ch, j)
                for j in range(4, MU):
                    sum_out(ch, j)

            def both(ch, odd):
                for j in range(4):
                    up_gate(ch - 1, j)
                project(ch)
                mean_squares(ch)
                for j in range(4):
                    sum_out(ch - 1, j)
                for j in range(4, MU):
                    up_gate(ch - 1, j)
                for j in range(4, MU):
                    sum_out(ch - 1, j)

            pe.wait_ge(fixed, 6)
            pe.wait_ge(w_hi, 3)
            pe.wait_ge(w_lo, 3)
            steps(pe, front, back, both)

        @block.vector
        def _(dve):
            for i, (lo, hi, raw) in enumerate(((qkvl, qkvh, raw_qkv), (swl, swh, raw_sw), (wol, woh, raw_wo))):
                dve.wait_ge(w_hi, i + 1)
                nc.vector.tensor_tensor(lo[:, :, :], raw, f32(hi[:, :, :]), ALU.subtract).then_inc(w_lo, 1)
            dve.sem_inc(xt_ready, 1)
            dve.sem_inc(dq, 1)
            dve.sem_inc(ao_done, 1)
            dve.sem_inc(f_done, 2)
            dve.wait_ge(fixed, 6)

            def normalise(ch):
                dve.wait_ge(x_in, ch * 16 + 16)
                for t in range(TC):
                    nc.vector.bn_stats(stats[:, t, :], xb[:, t, :]).then_inc(ln, 1)
                wait_alone(dve, passed["dve"], ln, ch * (3 * TC) + TC)
                for t in range(TC):
                    nc.vector.bn_aggr(mv[:, t, :], stats[:, t, :]).then_inc(ln, 1)
                dve.wait_ge(ln, ch * (3 * TC) + 2 * TC)
                dve.wait_ge(ln_pool, ch * 7 + 7)
                for t in range(TC):
                    nc.vector.tensor_scalar(xb[:, t, :], xb[:, t, :], mv[:, t, 0:1], s2[:, t:t + 1],
                                            ALU.subtract, ALU.mult).then_inc(ln, 1)

            def project(ch):
                for k in range(KE):
                    dve.wait_ge(xh_done, ch * KE + k + 1)
                    nc.vector.tensor_tensor(xl[:, k, :], ps[:, k, :], f32(xh[:, k, :]), ALU.subtract).then_inc(xl_done, 1)
                for k in range(KE):
                    dve.wait_ge(qkv_ready, ch * (3 * KE) + 2 * KE + k + 1)
                    nc.vector.tensor_copy(vv[:, k, :], ps[:, k, :]).then_inc(v_copied, 1)

            def cumulate(ch, odd):
                def wide(r):
                    return r.to_broadcast([P, KE, CW])

                for i, (t, r) in enumerate(((kk, rk), (qq, rq))):
                    dve.wait_ge(rms_done, ch * 2 + i + 1)
                    dve.wait_ge(kq_copied, ch * (2 * KE) + 2 * i + 2)
                    nc.vector.tensor_tensor(t, t, wide(r), ALU.mult).then_inc(scaled, 1)
                dve.wait_ge(exp_done, ch * 2 + 1)
                dve.wait_ge(v_copied, ch * KE + KE)
                nc.vector.tensor_tensor(vv, vv, kk, ALU.mult).then_inc(wv_done, 1)
                dve.wait_ge(ms_ready, ch * 2 + 2)
                if odd:
                    dve.wait_ge(carried, ch + 1)
                for i, (src, dst) in enumerate(((kk, wc), (vv, kc))):
                    if i:
                        dve.wait_ge(wv_done, ch + 1)
                    for k in range(KE):
                        nc.vector.tensor_tensor_scan(dst[:, k, :], ones[:, :], src[:, k, :],
                                                     carry[:, i, k:k + 1] if odd else 0.0, ALU.mult, ALU.add)\
                          .then_inc(scan_done, 1)

            def denominator(ch, odd):
                dve.wait_ge(plus_one, ch + 1)
                dve.wait_ge(scan_done, (ch + 1) * (2 * KE))
                if not odd:
                    for i, s in enumerate((wc, kc)):
                        nc.vector.tensor_copy(carry[:, i, :], s[:, :, CW - 1]).then_inc(carried, 1)
                nc.vector.scalar_tensor_tensor(qq, wc, CUM_EPS, qq, ALU.add, ALU.mult).then_inc(quotient, 1)

            def quotients(ch):
                dve.wait_ge(quotient, ch * 3 + 1)
                nc.vector.reciprocal(qq, qq).then_inc(quotient, 1)
                dve.wait_ge(quotient, ch * 3 + 2)
                nc.vector.tensor_tensor(qq, kc, qq, ALU.mult).then_inc(quotient, 1)

            def gate_values(ch):
                dve.wait_ge(codes_in, (ch + 1) * LOADS)
                if later(ch):
                    dve.wait_ge(gl_done, ch)
                dequantize(nc, dve, codes[:, :], scale_rows[:, :], bits, mag, mag, dq, ch * (NIBBLES * DQ_DVE) + 1)

            def times_up(ch, j):
                dve.wait_ge(silu_done, ch * MU + j + 1)
                nc.vector.tensor_tensor(sg[:, j % 2, :], ps[:, BANK_UG + 2 * (j % 2), :], sg[:, j % 2, :], ALU.mult)\
                  .then_inc(f_done, 1)

            def front(ch, odd):
                normalise(ch)
                project(ch)
                cumulate(ch, odd)
                denominator(ch, odd)
                quotients(ch)
                gate_values(ch)

            def back(ch, odd):
                for j in range(MU):
                    times_up(ch, j)

            def both(ch, odd):
                normalise(ch)
                for j in range(4):
                    times_up(ch - 1, j)
                project(ch)
                cumulate(ch, odd)
                for j in range(4, 6):
                    times_up(ch - 1, j)
                denominator(ch, odd)
                for j in range(6, MU):
                    times_up(ch - 1, j)
                quotients(ch)
                gate_values(ch)

            steps(dve, front, back, both)

def phase_b2(nc, x1, att, guh, gul, dn_codes, dn_scales, out):
    with ExitStack() as ctx:
        def sb(name, shape, dt=F32):
            return ctx.enter_context(nc.sbuf_tensor("c_" + name, shape, dt))

        def sem(name):
            return ctx.enter_context(nc.semaphore("c_" + name))

        TD = MF // NIBBLES
        TS_ = CW // E
        dnh, dnl = sb("dnh", [P, TD, NIBBLES, E], F32R), sb("dnl", [P, TD, NIBBLES, E], F32R)
        xh, xl = sb("xh", [P, 2, KE, CW], F32R), sb("xl", [P, 2, KE, CW], F32R)
        F_RING = 4
        fh, fl = sb("fh", [P, F_RING, CW], F32R), sb("fl", [P, F_RING, CW], F32R)
        gg = sb("gg", [P, F_RING, CW])
        xb = sb("xb", [P, TC, E])
        xn = sb("xn", [P, TC, NIBBLES, P])
        rr = sb("rr", [P, 2, TC, E])
        ab = sb("ab", [P, 2, KE, CW])
        ot = sb("ot", [P, KE, CW])
        oo = sb("oo", [P, TC, E])
        codes = sb("codes", [P, 2, CW], I32)
        scale_rows = sb("scale_rows", [P, 2, CW])
        bits, mag = sb("bits", [P, NIBBLES, CW], I32), sb("mag", [P, NIBBLES, CW])
        ident = sb("ident", [P, P])
        stats = sb("stats", [P, TC, 6])
        mv = sb("mv", [P, TC, 2])
        rstd, half = sb("rstd", [P, TC]), sb("half", [P, TC])
        ps = ctx.enter_context(nc.psum_tensor("c_ps", [P, 8, CW], F32))
        BANK_UG, BANK_OUT = 2, 6

        passed = {e: sem("passed_" + e) for e in ("dve", "pool")}
        fixed = sem("fixed")
        codes_in = [sem(f"codes_in{i}") for i in range(2)]
        dq, dh_done, dl_done = sem("dq"), sem("dh_done"), sem("dl_done")
        x_in = sem("x_in")
        ab_in = [sem(f"ab_in{i}") for i in range(2)]
        ln, ln_pool = sem("ln"), sem("ln_pool")
        xt_ready, xh_done, xl_done = sem("xt_ready"), sem("xh_done"), sem("xl_done")
        gu_ready, gelu_done, f_done = sem("gu_ready"), sem("gelu_done"), sem("f_done")
        fh_done, fl_done = sem("fh_done"), sem("fl_done")
        summed, ot_done, oo_ready, oo_done, oo_out = (sem("summed"), sem("ot_done"), sem("oo_ready"),
                                                      sem("oo_done"), sem("oo_out"))
        block = ctx.enter_context(nc.Block())

        @block.sync
        def _(sp):
            def load(ch, odd):
                sp.wait_ge(ln_pool, ch * 3 + 1)
                sp.wait_ge(ln, ch * (3 * TC) + 1)
                sp.dma_start(xb[:, :, :], x1[ch].rearrange("(t p) e -> p t e", p=P)).then_inc(x_in, 16)
                sp.wait_ge(ot_done, (ch - 1) * KE + 1)
                sp.dma_start(ab[:, odd, :, :], att[ch]).then_inc(ab_in[odd], 16)

            def store(ch, odd):
                sp.wait_ge(oo_done, (ch + 1) * TC)
                sp.dma_start(out[ch].rearrange("(t p) e -> p t e", p=P), oo[:, :, :]).then_inc(oo_out, 16)

            def both(ch, odd):
                load(ch, odd)
                store(ch - 1, 1 - odd)

            sp.sem_inc(oo_out, 1)
            for s in range(DN_SLICES):
                if s == 1:
                    sp.wait_ge(ln, 1)
                    sp.dma_start(xb[:, :, :], x1[0].rearrange("(t p) e -> p t e", p=P)).then_inc(x_in, 16)
                    sp.dma_start(ab[:, 0, :, :], att[0]).then_inc(ab_in[0], 16)
                if s >= 2:
                    sp.wait_ge(dq, (s - 1) * (NIBBLES * DQ_DVE))
                load_codes(sp, dn_codes[s], dn_scales[s], codes[:, s % 2, :], scale_rows[:, s % 2, :], codes_in[s % 2])
            steps(sp, lambda ch, odd: None, store, both)
            sp.wait_ge(oo_out, CHUNKS * 16 + 1)

        @block.gpsimd
        def _(pool):
            nc.gpsimd.memset(ident[:, :], 0.0).then_inc(fixed, 1)
            nc.gpsimd.memset(half[:, :], -0.5).then_inc(fixed, 1)
            pool.wait_ge(fixed, 2)
            nc.gpsimd.affine_select(out=ident[:, :], in_=ident[:, :], compare_op=ALU.not_equal, fill=1.0,
                                    base=0, pattern=[[-1, P]], channel_multiplier=1).then_inc(fixed, 1)

            def rstds(ch):
                wait_alone(pool, passed["pool"], ln, ch * (3 * TC) + 2 * TC + 1)
                nc.gpsimd.tensor_scalar(rstd[:, :], mv[:, :, 1], LN_EPS, None, ALU.add).then_inc(ln_pool, 1)
                pool.wait_ge(ln_pool, ch * 3 + 2)
                nc.gpsimd.tensor_tensor(rstd[:, :], rstd[:, :], half[:, :], ALU.pow).then_inc(ln_pool, 1)

            def residual(ch, odd):
                pool.wait_ge(ln, (ch + 1) * (3 * TC) + 1)
                nc.gpsimd.tensor_tensor(rr[:, odd, :, :].rearrange("p t (m e) -> p t m e", e=NIBBLES),
                                        xb[:, :, :].rearrange("p t (m e) -> p t m e", e=NIBBLES),
                                        xn[:, :, :, :].rearrange("p t e m -> p t m e"), ALU.add).then_inc(ln_pool, 1)

            def f_lo(ch, j):
                pool.wait_ge(fh_done, ch * MF + j + 1)
                nc.gpsimd.tensor_tensor(fl[:, j % F_RING, :], gg[:, j % F_RING, :], f32(fh[:, j % F_RING, :]), ALU.subtract)\
                  .then_inc(fl_done, 1)

            def front(ch, odd):
                rstds(ch)
                residual(ch, odd)
                for s in range(DN_SLICES):
                    pool.wait_ge(dh_done, s + 1)
                    r = slice(TS_ * s, TS_ * s + TS_)
                    nc.gpsimd.tensor_tensor(dnl[:, r, :, :], mag[:, :, :].rearrange("p e (t n) -> p t e n", t=TS_),
                                            f32(dnh[:, r, :, :]), ALU.subtract).then_inc(dl_done, 1)

            def back(ch, odd):
                for j in range(MF):
                    f_lo(ch, j)

            def both(ch, odd):
                for j in range(MF):
                    f_lo(ch - 1, j)
                    if j == 2:
                        rstds(ch)
                    if j == 6:
                        residual(ch, odd)

            steps(pool, front, back, both)

        @block.scalar
        def _(act):
            def x_hi(ch, odd, k):
                act.wait_ge(xt_ready, ch * KE + k + 1)
                nc.scalar.activation(xh[:, odd, k, :], ps[:, k, :], ACT.Copy).then_inc(xh_done, 1)

            def gelu(ch, j):
                act.wait_ge(gu_ready, ch * MF + j + 1)
                if j >= F_RING:
                    act.wait_ge(fl_done, ch * MF + j - F_RING + 1)
                nc.scalar.activation(gg[:, j % F_RING, :], ps[:, BANK_UG + 2 * (j % 2), :], ACT.Gelu_apprx_tanh)\
                  .then_inc(gelu_done, 1)

            def f_hi(ch, j):
                act.wait_ge(f_done, ch * MF + j + 3)
                if j >= F_RING:
                    act.wait_ge(summed, ch * MF + j - F_RING + 1)
                nc.scalar.activation(fh[:, j % F_RING, :], gg[:, j % F_RING, :], ACT.Copy).then_inc(fh_done, 1)

            def front(ch, odd):
                for k in range(KE):
                    x_hi(ch, odd, k)
                for s in range(DN_SLICES):
                    act.wait_ge(dq, (s + 1) * (NIBBLES * DQ_DVE))
                    nc.scalar.activation(dnh[:, TS_ * s:TS_ * s + TS_, :, :],
                                         mag[:, :, :].rearrange("p e (t n) -> p t e n", t=TS_), ACT.Copy).then_inc(dh_done, 1)

            def all_tiles(ch, between):
                for j in range(MF + 1):
                    if j < MF:
                        gelu(ch, j)
                    if j:
                        f_hi(ch, j - 1)
                    between(j)

            def back(ch, odd):
                all_tiles(ch, lambda j: None)

            def both(ch, odd):
                all_tiles(ch - 1, lambda j: x_hi(ch, odd, j - 9) if 9 <= j < 9 + KE else None)

            steps(act, front, back, both)

        @block.tensor
        def _(pe):
            def three(out, lh, ll, rh, rl, start, stop):
                nc.tensor.matmul(out, lh, rh, start=start, stop=False)
                nc.tensor.matmul(out, ll, rh, start=False, stop=False)
                return nc.tensor.matmul(out, lh, rl, start=False, stop=stop)

            def x_turn(ch):
                pe.wait_ge(ln, (ch + 1) * (3 * TC) + 1)
                for k in range(NIBBLES):
                    for t in range(TC):
                        mm = nc.tensor.transpose(ps[:, k, t * P:t * P + P], xn[:, t, k, :], ident[:, :])
                    mm.then_inc(xt_ready, 1)

            def gate_up(ch, odd, j):
                if j == 0:
                    pe.wait_ge(xl_done, (ch + 1) * KE)
                pe.wait_ge(f_done, ch * MF + j + 1)
                for i in range(2):
                    s, c = (i * MF + j) // TC, (j % TC) * P
                    for k in range(NIBBLES):
                        mm = three(ps[:, BANK_UG + 2 * (j % 2) + i, :], guh[:, s, k, c:c + P], gul[:, s, k, c:c + P],
                                   xh[:, odd, k, :], xl[:, odd, k, :], k == 0, k == NIBBLES - 1)
                mm.then_inc(gu_ready, 1)

            def sum_out(ch, j):
                pe.wait_ge(fl_done, ch * MF + j + 1)
                if j == 0:
                    pe.wait_ge(ot_done, ch * KE + 1)
                if j % (NIBBLES * TS_) == 0:
                    pe.wait_ge(dl_done, j // (NIBBLES * TS_) + 1)
                for i in range(KE):
                    w = slice(i * P, i * P + P)
                    mm = three(ps[:, BANK_OUT + i, :], dnh[:, j // 2, j % 2, w], dnl[:, j // 2, j % 2, w],
                               fh[:, j % F_RING, :], fl[:, j % F_RING, :], j == 0, j == MF - 1)
                mm.then_inc(summed, 1)

            def out_turn(ch, turned):
                pe.wait_ge(ot_done, (ch + 1) * KE + 1)
                pe.wait_ge(xl_done, turned * KE)
                for t in range(TC):
                    for k in range(KE):
                        mm = nc.tensor.transpose(ps[:, t // 2, (t % 2) * E + k * P:(t % 2) * E + k * P + P],
                                                 ot[:, k, t * P:t * P + P], ident[:, :])
                    if t % 2:
                        mm.then_inc(oo_ready, 1)

            LAG = 2

            def all_tiles(ch, odd, turned, between):
                for j in range(MF + LAG):
                    if j < MF:
                        gate_up(ch, odd, j)
                    if j >= LAG:
                        sum_out(ch, j - LAG)
                    between(j)
                out_turn(ch, turned)

            def back(ch, odd):
                all_tiles(ch, odd, ch + 1, lambda j: None)

            def both(ch, odd):
                all_tiles(ch - 1, 1 - odd, ch + 1, lambda j: x_turn(ch) if j == 8 else None)

            pe.wait_ge(fixed, 3)
            steps(pe, lambda ch, odd: x_turn(ch), back, both)

        @block.vector
        def _(dve):
            dve.sem_inc(ln, 1)
            dve.sem_inc(ln_pool, 1)
            dve.sem_inc(f_done, 2)
            dve.sem_inc(ot_done, 1)

            def normalise(ch):
                dve.wait_ge(x_in, ch * 16 + 16)
                for t in range(TC):
                    nc.vector.bn_stats(stats[:, t, :], xb[:, t, :]).then_inc(ln, 1)
                wait_alone(dve, passed["dve"], ln, ch * (3 * TC) + TC + 1)
                for t in range(TC):
                    nc.vector.bn_aggr(mv[:, t, :], stats[:, t, :]).then_inc(ln, 1)
                dve.wait_ge(ln, ch * (3 * TC) + 2 * TC + 1)

            def scale_rows_of(ch):
                dve.wait_ge(ln_pool, ch * 3 + 3)
                for t in range(TC):
                    nc.vector.tensor_scalar(xn[:, t, :, :], xb[:, t, :].rearrange("p (m e) -> p e m", e=NIBBLES),
                                            mv[:, t, 0:1], rstd[:, t:t + 1], ALU.subtract, ALU.mult).then_inc(ln, 1)

            def x_lo(ch, odd, k):
                dve.wait_ge(xh_done, ch * KE + k + 1)
                nc.vector.tensor_tensor(xl[:, odd, k, :], ps[:, k, :], f32(xh[:, odd, k, :]), ALU.subtract).then_inc(xl_done, 1)

            def times_up(ch, j):
                dve.wait_ge(gelu_done, ch * MF + j + 1)
                nc.vector.tensor_tensor(gg[:, j % F_RING, :], ps[:, BANK_UG + 2 * (j % 2) + 1, :], gg[:, j % F_RING, :], ALU.mult)\
                  .then_inc(f_done, 1)

            def finish(ch, odd):
                dve.wait_ge(summed, (ch + 1) * MF)
                dve.wait_ge(ab_in[odd], (ch - odd + 2) * 8)
                for k in range(KE):
                    nc.vector.tensor_tensor(ot[:, k, :], ps[:, BANK_OUT + k, :], ab[:, odd, k, :], ALU.add).then_inc(ot_done, 1)
                for i in range(2):
                    dve.wait_ge(oo_ready, ch * 2 + i + 1)
                    if i == 0:
                        dve.wait_ge(oo_out, ch * 16 + 1)
                        dve.wait_ge(ln_pool, ch * 3 + 4)
                    for t in range(2 * i, 2 * i + 2):
                        nc.vector.tensor_tensor(oo[:, t, :], ps[:, i, (t % 2) * E:(t % 2) * E + E], rr[:, odd, t, :], ALU.add)\
                          .then_inc(oo_done, 1)

            def front(ch, odd):
                normalise(ch)
                scale_rows_of(ch)
                for k in range(KE):
                    x_lo(ch, odd, k)
                for s in range(DN_SLICES):
                    dve.wait_ge(codes_in[s % 2], (s // 2 + 1) * LOADS)
                    if s:
                        dve.wait_ge(dl_done, s)
                    dequantize(nc, dve, codes[:, s % 2, :], scale_rows[:, s % 2, :], bits, mag, mag, dq, s * (NIBBLES * DQ_DVE))

            def back(ch, odd):
                for j in range(MF):
                    times_up(ch, j)
                finish(ch, odd)

            def both(ch, odd):
                for j in range(MF):
                    times_up(ch - 1, j)
                    if j == 1:
                        normalise(ch)
                    if j == 5:
                        scale_rows_of(ch)
                    if 9 <= j < 9 + KE:
                        x_lo(ch, odd, j - 9)
                finish(ch - 1, 1 - odd)

            steps(dve, front, back, both)

def build(nc, d):
    x1 = nc.dram_tensor("x1_scratch", [CHUNKS, CW, E], F32, kind="Internal").ap()
    att = nc.dram_tensor("att_scratch", [CHUNKS, P, KE, CW], F32, kind="Internal").ap()
    phase_a(nc, d["x"], d["w0"], d["w_bin"], d["bias_cols"], d["bias_rows"], d["rope"],
            x1.rearrange("(b c) t e -> b (c t) e", b=B))
    with ExitStack() as ctx:
        guh, gul = (ctx.enter_context(nc.sbuf_tensor(name, [P, GU_SLICES, NIBBLES, CW], F32R)) for name in ("guh", "gul"))
        phase_b1(nc, x1, d["w_qkv"], d["w_swiglu"], d["w_out"], d["gu_codes"], d["gu_scales"], guh, gul, att)
        phase_b2(nc, x1, att, guh, gul, d["dn_codes"], d["dn_scales"], d["out"])


def rope_tables():
    inv = (1.0 / np.float32(10000.0) ** (np.arange(0, D, 2, dtype=np.float32) / np.float32(D))).astype(np.float32)
    angle = np.arange(S, dtype=np.float32)[None, :] * inv[np.arange(P) % (D // 2)][:, None]
    sign = np.where(np.arange(P) % D < D // 2, -1.0, 1.0).astype(np.float32)[:, None]
    return np.stack([np.cos(angle), np.sin(angle) * sign]).astype(np.float32)


def swap_halves(a):
    return np.roll(a.reshape(-1, D, *a.shape[1:]), D // 2, axis=1).reshape(a.shape)


def gate_columns(a):
    rows = a.shape[0]
    a = a.reshape(rows, MLP // (NIBBLES * P), P, NIBBLES).transpose(0, 1, 3, 2).reshape(rows, MLP // CW, CW)
    return a.transpose(1, 0, 2)


def down_slices(a, rows):
    return a.reshape(DN_SLICES, CW // E, rows, E).transpose(0, 2, 1, 3).reshape(DN_SLICES, rows, CW)


def lay_out(i):
    wq, wk, bq, bk = i["L0_attn_wq"], i["L0_attn_wk"], i["L0_attn_bq"], i["L0_attn_bk"]
    wo = i["L0_attn_wo"].T.reshape(KV // 2, 2, G, D, E).transpose(0, 2, 1, 3, 4).reshape(E, E)
    bqr, bkr = swap_halves(bq), swap_halves(bk)
    return {
        "x": i["L0_attn_x"],
        "w0": np.concatenate([wq.T, swap_halves(wq).T, wk.T, i["L0_attn_wv"].T, swap_halves(wk).T, wo], axis=1),
        "w_bin": i["L0_ffn_weight"],
        "bias_cols": np.stack([bq[:P], bq[P:], bqr[:P], bqr[P:], np.concatenate([bk, i["L0_attn_bv"]]),
                               np.concatenate([bkr, bkr])], axis=1),
        "bias_rows": np.stack([i["L0_attn_bo"], i["L0_ffn_bias"]]),
        "rope": rope_tables(),
        "w_qkv": i["L1_attn_w_qkv"].T,
        "w_swiglu": i["L1_attn_w_swiglu"].T,
        "w_out": i["L1_attn_w_out"].T,
        "gu_codes": np.concatenate([gate_columns(i["L1_ffn_gate_W_packed"].T), gate_columns(i["L1_ffn_up_W_packed"].T)]),
        "gu_scales": np.concatenate([gate_columns(i["L1_ffn_gate_scales"].T), gate_columns(i["L1_ffn_up_scales"].T)]),
        "dn_codes": down_slices(i["L1_ffn_down_W_packed"].T, P),
        "dn_scales": down_slices(i["L1_ffn_down_scales"].T, P // BLOCK_ROWS),
    }


def kernel(**inputs):
    import concourse.bacc as bacc
    from concourse.bass_utils import run_bass_kernel_spmd

    nc = bacc.Bacc("TRN2", target_bir_lowering=False, num_devices=1)
    arrays, dram = {}, {}
    for name, a in lay_out({k: np.asarray(v) for k, v in inputs.items()}).items():
        arrays[f"in_{name}"] = np.ascontiguousarray(a)
        dram[name] = nc.dram_tensor(f"in_{name}", a.shape, mybir.dt.from_np(a.dtype), kind="ExternalInput").ap()
    dram["out"] = nc.dram_tensor("out_0", (CHUNKS, CW, E), F32, kind="ExternalOutput").ap()
    build(nc, dram)
    r = run_bass_kernel_spmd(nc, [arrays], core_ids=[0])
    return r.results[0]["out_0"].reshape(B, S, E)
```

```python
from contextlib import ExitStack

import numpy as np

import concourse.bass as bass
from concourse import mybir

ALU = mybir.AluOpType
ACT = mybir.ActivationFunctionType
AX_X = mybir.AxisListType.X
F32 = mybir.dt.float32
F32R = mybir.dt.float32r
BF16 = mybir.dt.bfloat16
I32 = mybir.dt.int32

P = 128
B, S, E = 4, 1024, 256
KE = E // P
H, KV, D = 16, 4, 16
G = H // KV
TT = S // P
CW = 512
NC = S // CW
TC = CW // P
LN_EPS = 1e-5

PIECES = 3
STACK = PIECES * D
PAIR = 2 * STACK
SHIFT = PAIR
ROWS = PAIR + 2


def f32(ap):
    return ap.bitcast(F32)


def wait_alone(engine, passed, sem, value):
    engine.wait_ge(sem, value)
    engine.sem_inc(passed, 1)



W_Q = 0
W_QR = W_Q + E
W_K = W_QR + E
W_KR = W_K + 2 * KV * D
W_O = W_KR + KV * D
W_ALL0 = W_O + E
W_BIN = W_O

TILES = [(W_K, 2 * KV * D), (W_KR, KV * D), (W_Q, P), (W_QR, P), (W_Q + P, P), (W_QR + P, P)]
ROT = [(KV * D, 4, 5), (P, 0, 2), (P, 1, 3)]
NR = len(ROT)
BANK_P = 2
LN_SIGNALS = 5


def steps(engine, front, back, both):
    front(0, 0)
    with engine.Fori(0, B - 1) as b:
        both(2 * b + 1, 1)
        both(2 * b + 2, 0)
    both(B * NC - 1, 1)
    back(B * NC - 1, 1)


def later(ch):
    return not isinstance(ch, int) or ch > 0


QK_STORES = 2 * NR * 16


def three(nc, out, lh, ll, rh, rl, start, stop):
    nc.tensor.matmul(out, lh, rh, start=start, stop=False)
    nc.tensor.matmul(out, ll, rh, start=False, stop=False)
    return nc.tensor.matmul(out, lh, rl, start=False, stop=stop)


def load_group(sp, scratch, qs, ks, vv, b, g, group_in, part):
    if part == 0:
        for half in range(2):
            for piece, hilo in enumerate((0, 0, 1)):
                r = STACK * half + D * piece
                sp.dma_start(f32(ks[r:r + D, half, g, :]), scratch["k"][b, hilo, D * g:D * g + D, :]).then_inc(group_in[g], 16)
        return
    for half in range(2):
        for piece, hilo in enumerate((0, 1, 0)):
            r = STACK * half + D * piece
            heads = scratch["q"][b, hilo, G * D * g:G * D * (g + 1), :].rearrange("(j i d) s -> i d j s", j=2, i=2)
            sp.dma_start(f32(qs[r:r + D, 2 * g:2 * g + 2, :]), heads[half]).then_inc(group_in[g], 16)
    sp.dma_start(vv[:, g, :, :].rearrange("p (c t) d -> p c (t d)", c=NC),
                 scratch["v"][b, :, :, g].rearrange("c p t d -> p c (t d)")).then_inc(group_in[g], 16)


GROUP_LOADS = 16 * (2 * 2 * PIECES + 1)


def phase_a1(nc, x, w0, w_bin, bias_cols, bias_rows, rope, scratch, kept):
    with ExitStack() as ctx:
        def sb(name, shape, dt=F32):
            return ctx.enter_context(nc.sbuf_tensor("a_" + name, shape, dt))

        def sem(name):
            return ctx.enter_context(nc.semaphore("a_" + name))

        ident, identb, future, woh, wol, qs, ks, vv, group_in = (kept[n] for n in
            ("ident", "identb", "future", "woh", "wol", "qs", "ks", "vv", "group_in"))
        wh, wl = sb("wh", [P, KE, W_ALL0], F32R), sb("wl", [P, KE, W_ALL0], F32R)
        raw = sb("raw", [P, KE, W_ALL0])
        wb = sb("wb", [P, KE, E])
        wt = sb("wt", [P, KE, E])
        wabs = sb("wabs", [P, KE, 1])
        bcol = sb("bcol", [P, 6])
        brow = sb("brow", [P, 2, E])
        bsum = sb("bsum", [P, E])
        cos, sin = sb("cos", [P, S]), sb("sin", [P, S])
        xb = sb("xb", [P, 2, TC, E])
        xr = sb("xr", [P, 2, TC, E])
        xn = sb("xn", [P, TC, E])
        stats, mv = sb("stats", [P, TC, 6]), sb("mv", [P, TC, 2])
        rstd, shift, half = sb("rstd", [P, TC]), sb("shift", [P, TC]), sb("half", [P, TC])
        xh, xl = sb("xh", [P, 2, KE, CW], F32R), sb("xl", [P, 2, KE, CW], F32R)
        t1, t2 = sb("t1", [P, CW]), sb("t2", [P, CW])
        qf = sb("qf", [P, NR, CW])
        qh, ql = sb("qh", [P, 2, NR, CW], F32R), sb("ql", [P, 2, NR, CW], F32R)
        vt = sb("vt", [P, CW])
        vo = sb("vo", [P, 2, KV, TC, 2 * D])
        ps = ctx.enter_context(nc.psum_tensor("a_ps", [P, 8, CW], F32))
        wabs_out = qf[:, 0:KE, 0:E]
        ones = f32(ql[0:1, 1, 0:NC, :]).rearrange("p c s -> p (c s)")

        passed = {e: sem("passed_" + e) for e in ("sp", "pe", "dve", "pool")}
        w_in, bin_in, k_one = sem("w_in"), sem("bin_in"), sem("k_one")
        w_abs, w_bw, w_bt, w_hi, w_lo = sem("w_abs"), sem("w_bw"), sem("w_bt"), sem("w_hi"), sem("w_lo")
        const, fixed = sem("const"), sem("fixed")
        x_in, qk_out, v_out, xr_out = ([sem(f"{n}{i}") for i in range(2)] for n in ("x_in", "qk_out", "v_out", "xr_out"))
        ln, ln_pool, xn_done = sem("ln"), sem("ln_pool"), sem("xn_done")
        xt_ready, xh_done, xl_done = sem("xt_ready"), sem("xh_done"), sem("xl_done")
        proj_ready, rope_done = sem("proj_ready"), sem("rope_done")
        qh_done, ql_done = sem("qh_done"), sem("ql_done")
        v_done, vt_ready, vo_done = sem("v_done"), sem("vt_ready"), sem("vo_done")
        bin_ready, x_added = sem("bin_ready"), sem("x_added")

        def of_parity(ch, odd, each):
            return (ch - odd) * (each // 2)

        block = ctx.enter_context(nc.Block())

        @block.sync
        def _(sp):
            def load(ch, odd):
                wait_alone(sp, passed["sp"], xn_done, (ch + 1) * TC)
                wait_alone(sp, passed["sp"], ln_pool, (ch + 1) * LN_SIGNALS)
                sp.dma_start(xb[:, odd, :, :], x[ch].rearrange("(t p) e -> p t e", p=P)).then_inc(x_in[odd], 16)

            load(0, 0)
            sp.dma_start(raw[:, :, :], w0.rearrange("(k p) n -> p k n", p=P)).then_inc(w_in, 16)
            sp.dma_start(wb[:, :, :], w_bin.rearrange("(k p) n -> p k n", p=P)).then_inc(bin_in, 16)
            load(1, 1)
            sp.dma_start(bcol[:, :], bias_cols).then_inc(const, 16)
            for r in range(2):
                sp.dma_start(brow[:, r, :], bias_rows[r:r + 1, :].to_broadcast([P, E])).then_inc(const, 16)
            sp.dma_start(cos[:, :], rope[0]).then_inc(const, 16)
            sp.dma_start(sin[:, :], rope[1]).then_inc(const, 16)
            sp.wait_ge(fixed, 7)
            for half_ in range(2):
                for g in range(KV):
                    sp.dma_start(f32(ks[SHIFT + half_:SHIFT + half_ + 1, half_, g, :]), ones).then_inc(k_one, 16)

            def store(b, odd):
                ch = NC * b + odd
                for r in range(NR):
                    rows = ROT[r][0]
                    first = max(0, r - 1) * P
                    dst = scratch["q" if r else "k"][b, :, first:first + rows, odd * CW:odd * CW + CW]
                    wait_alone(sp, passed["sp"], qh_done, ch * NR + r + 1)
                    sp.dma_start(dst[0], f32(qh[0:rows, odd, r, :])).then_inc(qk_out[odd], 16)
                    wait_alone(sp, passed["sp"], ql_done, (ch + 1) * NR + r + 1)
                    sp.dma_start(dst[1], f32(ql[0:rows, odd, r, :])).then_inc(qk_out[odd], 16)
                wait_alone(sp, passed["sp"], vo_done, ch + 2)
                sp.dma_start(scratch["v"][b, odd], vo[:, odd, :, :, :]).then_inc(v_out[odd], 16)
                wait_alone(sp, passed["sp"], x_added, (ch + 2) * 2)
                sp.dma_start(scratch["xr"][b, odd].rearrange("(t p) e -> p t e", p=P), xr[:, odd, :, :]).then_inc(xr_out[odd], 16)

            with sp.Fori(0, B - 1) as b:
                for odd in range(NC):
                    load(NC * b + odd + 2, odd)
                    store(b, odd)
            store(B - 1, 0)
            for odd in range(NC):
                sp.wait_ge(qk_out[odd], 2 * QK_STORES)
                sp.wait_ge(v_out[odd], 2 * 16)
            sp.wait_ge(k_one, 2 * KV * 16)
            for part in range(2):
                load_group(sp, scratch, qs, ks, vv, 0, 0, group_in, part)
            store(B - 1, 1)
            for odd in range(NC):
                sp.wait_ge(qk_out[odd], (B + 1) * QK_STORES)
                sp.wait_ge(v_out[odd], (B + 1) * 16)
                sp.wait_ge(xr_out[odd], (B + 1) * 16)

        @block.gpsimd
        def _(pool):
            nc.gpsimd.memset(ident[:, :], 0.0).then_inc(fixed, 1)
            nc.gpsimd.memset(future[:, :], 0.0).then_inc(fixed, 1)
            nc.gpsimd.memset(half[:, :], -0.5).then_inc(fixed, 1)
            nc.gpsimd.memset(ones, 1.0).then_inc(fixed, 1)
            pool.wait_ge(fixed, 4)
            nc.gpsimd.affine_select(out=ident[:, :], in_=ident[:, :], compare_op=ALU.not_equal, fill=1.0,
                                    base=0, pattern=[[-1, P]], channel_multiplier=1).then_inc(fixed, 1)
            nc.gpsimd.affine_select(out=future[:, :], in_=future[:, :], compare_op=ALU.is_ge, fill=-1e30,
                                    base=0, pattern=[[-1, P]], channel_multiplier=1).then_inc(fixed, 1)

            def norm_scales(ch, odd):
                at = (ch + 2) * LN_SIGNALS
                wait_alone(pool, passed["pool"], ln, (ch + 1) * 2 * TC)
                wait_alone(pool, passed["pool"], xn_done, (ch + 2) * TC)
                nc.gpsimd.tensor_scalar(rstd[:, :], mv[:, :, 1], LN_EPS, None, ALU.add).then_inc(ln_pool, 1)
                pool.wait_ge(ln_pool, at + 1)
                nc.gpsimd.tensor_tensor(rstd[:, :], rstd[:, :], half[:, :], ALU.pow).then_inc(ln_pool, 1)
                wait_alone(pool, passed["pool"], ln_pool, at + 2)
                nc.gpsimd.tensor_scalar(shift[:, :], mv[:, :, 0], -1.0, None, ALU.mult).then_inc(ln_pool, 1)
                pool.wait_ge(ln_pool, at + 3)
                nc.gpsimd.tensor_tensor(shift[:, :], shift[:, :], rstd[:, :], ALU.mult).then_inc(ln_pool, 1)

            def biased(ch, odd):
                pool.wait_ge(xr_out[odd], of_parity(ch, odd, 16) + 16)
                nc.gpsimd.tensor_tensor(xr[:, odd, :, :], xb[:, odd, :, :], bsum[:, None, :].to_broadcast([P, TC, E]),
                                        ALU.add).then_inc(ln_pool, 1)

            def lo_part(ch, odd, r):
                rows = ROT[r][0]
                pool.wait_ge(qh_done, ch * NR + r + 1)
                nc.gpsimd.tensor_tensor(ql[0:rows, odd, r, :], qf[0:rows, r, :], f32(qh[0:rows, odd, r, :]),
                                        ALU.subtract).then_inc(ql_done, 1)

            def front(ch, odd):
                norm_scales(ch, odd)
                nc.gpsimd.memset(f32(ks[:, :, :, :]), 0.0).then_inc(fixed, 1)
                nc.gpsimd.memset(vo[:, :, :, :, :], 1.0).then_inc(fixed, 1)
                pool.wait_ge(const, 5 * 16)
                nc.gpsimd.tensor_tensor(bsum[:, :], brow[:, 0, :], brow[:, 1, :], ALU.add).then_inc(fixed, 1)
                pool.wait_ge(fixed, 9)
                biased(ch, odd)
                pool.wait_ge(k_one, 2 * KV * 16)

            def back(ch, odd):
                for r in range(NR):
                    lo_part(ch, odd, r)

            def both(ch, odd):
                norm_scales(ch, odd)
                lo_part(ch - 1, 1 - odd, 0)
                biased(ch, odd)
                for r in range(1, NR):
                    lo_part(ch - 1, 1 - odd, r)

            steps(pool, front, back, both)

        @block.scalar
        def _(act):
            def weights_hi():
                act.wait_ge(w_in, 16)
                nc.scalar.activation(wh[:, :, 0:W_O], raw[:, :, 0:W_O], ACT.Copy).then_inc(w_hi, 1)
                nc.scalar.activation(woh[:, :, :], raw[:, :, W_O:W_ALL0], ACT.Copy).then_inc(w_hi, 1)
                act.wait_ge(bin_in, 16)
                for k in range(KE):
                    nc.scalar.activation(wabs_out[:, k, :], wb[:, k, :], ACT.Abs, accum_out=wabs[:, k, :]).then_inc(w_abs, 1)
                nc.scalar.activation(identb[:, :], ident[:, :], ACT.Copy).then_inc(w_hi, 1)
                for k in range(KE):
                    act.wait_ge(w_bt, k + 1)
                    nc.scalar.activation(wh[:, k, W_BIN:W_BIN + E], ps[:, BANK_P + k, 0:E], ACT.Copy).then_inc(w_hi, 1)
                act.wait_ge(const, 5 * 16)
                act.wait_ge(fixed, 9)

            def normalise(ch, odd):
                act.wait_ge(ln_pool, (ch + 2) * LN_SIGNALS + 4)
                act.wait_ge(xt_ready, (ch + 1) * KE)
                for t in range(TC):
                    nc.scalar.activation(xn[:, t, :], xb[:, odd, t, :], ACT.Identity, bias=shift[:, t:t + 1],
                                         scale=rstd[:, t:t + 1]).then_inc(xn_done, 1)

            def x_hi(ch, odd):
                for k in range(KE):
                    act.wait_ge(xt_ready, (ch + 1) * KE + k + 1)
                    act.wait_ge(bin_ready, (ch + 1) * 2)
                    nc.scalar.activation(xh[:, odd, k, :], ps[:, k, :], ACT.Copy).then_inc(xh_done, 1)

            def values(ch, odd):
                act.wait_ge(proj_ready, ch * len(TILES) + 1)
                act.wait_ge(vt_ready, ch + 1)
                nc.scalar.activation(vt[KV * D:P, :], ps[KV * D:P, BANK_P, :], ACT.Identity,
                                     bias=bcol[KV * D:P, 4:5]).then_inc(v_done, 1)

            def values_by_key(ch, odd):
                act.wait_ge(vt_ready, ch + 2)
                act.wait_ge(v_out[odd], of_parity(ch, odd, 16) + 16)
                nc.scalar.activation(vo[:, odd, :, :, 0:D].rearrange("p g t d -> p t g d"),
                                     ps[:, BANK_P + 2, 0:TC * KV * D].rearrange("p (t g d) -> p t g d", g=KV, d=D),
                                     ACT.Copy).then_inc(vo_done, 1)

            def hi_part(ch, odd, r):
                rows = ROT[r][0]
                act.wait_ge(rope_done, ch * (3 * NR) + 3 * r + 4)
                act.wait_ge(qk_out[odd], of_parity(ch, odd, QK_STORES) + QK_STORES)
                nc.scalar.activation(qh[0:rows, odd, r, :], qf[0:rows, r, :], ACT.Copy).then_inc(qh_done, 1)

            def front(ch, odd):
                act.wait_ge(fixed, 5)
                normalise(ch, odd)
                x_hi(ch, odd)
                weights_hi()

            def back(ch, odd):
                values(ch, odd)
                for r in range(NR):
                    hi_part(ch, odd, r)
                values_by_key(ch, odd)

            def both(ch, odd):
                values(ch - 1, 1 - odd)
                normalise(ch, odd)
                hi_part(ch - 1, 1 - odd, 0)
                x_hi(ch, odd)
                for r in range(1, NR):
                    hi_part(ch - 1, 1 - odd, r)
                values_by_key(ch - 1, 1 - odd)

            steps(act, front, back, both)

        @block.tensor
        def _(pe):
            def front(ch, odd):
                pe.wait_ge(fixed, 5)
                turn(ch, odd)
                pe.wait_ge(w_bw, 7)
                for k in range(KE):
                    for o in range(KE):
                        mm_ = nc.tensor.transpose(ps[:, BANK_P + k, o * P:o * P + P], wt[:, o, k * P:k * P + P], ident[:, :])
                    mm_.then_inc(w_bt, 1)
                pe.wait_ge(w_hi, 3 + KE)
                pe.wait_ge(w_lo, 2 + KE)

            def turn(ch, odd):
                pe.wait_ge(xn_done, (ch + 3) * TC)
                pe.wait_ge(xl_done, (ch + 1) * KE)
                for k in range(KE):
                    for t in range(TC):
                        mm_ = nc.tensor.transpose(ps[:, k, t * P:t * P + P], xn[:, t, k * P:k * P + P], ident[:, :])
                    mm_.then_inc(xt_ready, 1)

            def project(ch, odd, js):
                for j in js:
                    w, cols = TILES[j]
                    if j == 0:
                        pe.wait_ge(xl_done, (ch + 2) * KE)
                        pe.wait_ge(x_added, ch * 2 + 1)
                    if j == 1:
                        pe.wait_ge(x_added, ch * 2 + 2)
                    if j == 2:
                        pe.wait_ge(vo_done, ch + 1)
                    if j >= 2:
                        pe.wait_ge(rope_done, ch * (3 * NR) + 1)
                    for k in range(KE):
                        mm_ = three(nc, ps[0:cols, BANK_P + j, :], wh[:, k, w:w + cols], wl[:, k, w:w + cols],
                                    xh[:, odd, k, :], xl[:, odd, k, :], k == 0, k == KE - 1)
                    mm_.then_inc(proj_ready, 1)

            def binarized(ch, odd):
                pe.wait_ge(rope_done, ch * (3 * NR) + 4)
                wait_alone(pe, passed["pe"], v_done, ch + 1)
                for h in range(2):
                    for t in (2 * h, 2 * h + 1):
                        r = slice(t * P, t * P + P)
                        for k in range(KE):
                            mm_ = three(nc, ps[:, BANK_P + h, (t % 2) * E:(t % 2) * E + E],
                                        xh[:, odd, k, r], xl[:, odd, k, r], wh[:, k, W_BIN:W_BIN + E],
                                        wl[:, k, W_BIN:W_BIN + E], k == 0, k == KE - 1)
                    mm_.then_inc(bin_ready, 1)

            def turn_values(ch, odd):
                wait_alone(pe, passed["pe"], rope_done, ch * (3 * NR) + 5)
                for t in range(TC):
                    mm_ = nc.tensor.transpose(ps[:, BANK_P + 2, t * KV * D:(t + 1) * KV * D], vt[KV * D:P, t * P:t * P + P],
                                              ident[KV * D:P, KV * D:P])
                mm_.then_inc(vt_ready, 1)

            def back(ch, odd):
                project(ch, odd, range(6))
                binarized(ch, odd)
                turn_values(ch, odd)

            def both(ch, odd):
                project(ch - 1, 1 - odd, range(5))
                turn(ch, odd)
                project(ch - 1, 1 - odd, range(5, 6))
                binarized(ch - 1, 1 - odd)
                turn_values(ch - 1, 1 - odd)

            steps(pe, front, back, both)

        @block.vector
        def _(dve):
            dve.sem_inc(xn_done, 2 * TC)
            dve.sem_inc(ln_pool, 2 * LN_SIGNALS)
            for odd in range(2):
                dve.sem_inc(xr_out[odd], 16)
                dve.sem_inc(qk_out[odd], QK_STORES)
                dve.sem_inc(v_out[odd], 16)
            dve.sem_inc(xt_ready, KE)
            dve.sem_inc(bin_ready, 2 * 2)
            dve.sem_inc(xl_done, KE)
            dve.sem_inc(x_added, 2)
            dve.sem_inc(vo_done, 1)
            dve.sem_inc(rope_done, 1)
            dve.sem_inc(vt_ready, 1)
            dve.sem_inc(ql_done, NR)

            def weights():
                dve.wait_ge(bin_in, 16)
                for k in range(KE):
                    nc.vector.tensor_scalar(wt[:, k, :], wb[:, k, :], 0.0, 2.0, ALU.is_ge, ALU.mult).then_inc(w_bw, 1)
                dve.wait_ge(w_abs, KE)
                nc.vector.tensor_scalar(wabs[:, :, :], wabs[:, :, :], 1.0 / E, None, ALU.mult).then_inc(w_bw, 1)
                dve.wait_ge(w_bw, KE + 1)
                for k in range(KE):
                    nc.vector.tensor_scalar(wt[:, k, :], wt[:, k, :], -1.0, wabs[:, k, :], ALU.add, ALU.mult).then_inc(w_bw, 1)
                dve.wait_ge(w_bw, 2 * KE + 1)
                nc.vector.tensor_tensor(wt[:, :, :], wt[:, :, :], wb[:, :, :], ALU.subtract).then_inc(w_bw, 1)
                dve.wait_ge(w_bw, 2 * KE + 2)
                nc.vector.tensor_tensor(wt[:, :, :], wt[:, :, :], wb[:, :, :], ALU.add).then_inc(w_bw, 1)
                dve.wait_ge(w_hi, 2)
                nc.vector.tensor_tensor(wl[:, :, 0:W_O], raw[:, :, 0:W_O], f32(wh[:, :, 0:W_O]), ALU.subtract).then_inc(w_lo, 1)
                for k in range(KE):
                    dve.wait_ge(w_hi, 4 + k)
                    nc.vector.tensor_tensor(wl[:, k, W_BIN:W_BIN + E], ps[:, BANK_P + k, 0:E], f32(wh[:, k, W_BIN:W_BIN + E]),
                                            ALU.subtract).then_inc(w_lo, 1)
                nc.vector.tensor_tensor(wol[:, :, :], raw[:, :, W_O:W_ALL0], f32(woh[:, :, :]), ALU.subtract).then_inc(w_lo, 1)
                dve.wait_ge(const, 5 * 16)

            def statistics(ch, odd):
                dve.wait_ge(x_in[odd], of_parity(ch, odd, 16) + 16)
                dve.wait_ge(ln_pool, (ch + 1) * LN_SIGNALS + 4)
                for t in range(TC):
                    nc.vector.bn_stats(stats[:, t, :], xb[:, odd, t, :]).then_inc(ln, 1)
                wait_alone(dve, passed["dve"], ln, ch * 2 * TC + TC)
                for t in range(TC):
                    nc.vector.bn_aggr(mv[:, t, :], stats[:, t, :]).then_inc(ln, 1)

            def x_lo(ch, odd):
                for k in range(KE):
                    dve.wait_ge(xh_done, ch * KE + k + 1)
                    nc.vector.tensor_tensor(xl[:, odd, k, :], ps[:, k, :], f32(xh[:, odd, k, :]), ALU.subtract).then_inc(xl_done, 1)

            def rotate(ch, odd, r):
                rows, b0, b1 = ROT[r]
                cols = slice(odd * CW, odd * CW + CW)
                before = ch * (3 * NR) + 3 * r + 1
                dve.wait_ge(proj_ready, ch * len(TILES) + 2 * r + 1)
                dve.wait_ge(rope_done, before)
                nc.vector.scalar_tensor_tensor(t1[0:rows], ps[0:rows, BANK_P + 2 * r, :], bcol[0:rows, b0:b0 + 1],
                                               cos[0:rows, cols], ALU.add, ALU.mult).then_inc(rope_done, 1)
                dve.wait_ge(proj_ready, ch * len(TILES) + 2 * r + 2)
                nc.vector.scalar_tensor_tensor(t2[0:rows], ps[0:rows, BANK_P + 2 * r + 1, :], bcol[0:rows, b1:b1 + 1],
                                               sin[0:rows, cols], ALU.add, ALU.mult).then_inc(rope_done, 1)
                dve.wait_ge(rope_done, before + 2)
                dve.wait_ge(ql_done, ch * NR + r + 1)
                nc.vector.tensor_tensor(qf[0:rows, r, :], t1[0:rows], t2[0:rows], ALU.add).then_inc(rope_done, 1)

            def add_binarized(ch, odd):
                dve.wait_ge(ln_pool, (ch + 3) * LN_SIGNALS)
                for h in range(2):
                    dve.wait_ge(bin_ready, ch * 2 + h + 5)
                    nc.vector.tensor_tensor(xr[:, odd, 2 * h:2 * h + 2, :],
                                            ps[:, BANK_P + h, :].rearrange("p (t e) -> p t e", e=E),
                                            xr[:, odd, 2 * h:2 * h + 2, :], ALU.add).then_inc(x_added, 1)

            def front(ch, odd):
                statistics(ch, odd)
                x_lo(ch, odd)
                weights()

            def back(ch, odd):
                for r in range(NR):
                    rotate(ch, odd, r)
                add_binarized(ch, odd)

            def both(ch, odd):
                statistics(ch, odd)
                rotate(ch - 1, 1 - odd, 0)
                rotate(ch - 1, 1 - odd, 1)
                x_lo(ch, odd)
                rotate(ch - 1, 1 - odd, 2)
                add_binarized(ch - 1, 1 - odd)

            steps(dve, front, back, both)

ITEMS = [(g, c) for g in range(KV) for c in range(NC)]
NI = len(ITEMS)
LOOKAHEAD = 2
LAG = 2
P_SLOTS = 4
NORM = 3
OUT_UNITS = TC // 2


def key_tiles(n):
    c = ITEMS[n % NI][1]
    return [(kt, max(0, kt - TC * c) * P, kt >= TC * c) for kt in range(TC * (c + 1))]


def max_units(n):
    c = ITEMS[n % NI][1]
    out = []
    for qt in range(TC * c, TC * c + TC):
        width = (qt + 1) * P
        for pair in range(2):
            out += [(qt, pair, k0, min(CW, width - k0)) for k0 in range(0, width, CW)]
    return out


def groups_before(n):
    return sum(len(key_tiles(m)) for m in range(n))


def group_at(k):
    n = 0
    while k >= len(key_tiles(n)):
        k -= len(key_tiles(n))
        n += 1
    return n, k


def diagonals_upto(k):
    return sum(key_tiles(n)[j][2] for n, j in map(group_at, range(k + 1)))


def step_units(n, ahead, out):
    units = []
    if ahead:
        units = [(i // 2, i % 2, n + LOOKAHEAD, u) for i, u in enumerate(max_units(n + LOOKAHEAD))]
    if out and n % NI == NI - 1:
        units += [(j, 3, None, (0, h)) for h, j in enumerate((6, 7))]
    if out and n % NI == 1:
        units += [(j, 3, None, (1, h)) for h, j in enumerate((1, 3))]
    return sorted(units, key=lambda unit: unit[0:2])


def hi_lo_after(n):
    return len(key_tiles(n)) - 1 if len(key_tiles(n)) == TC else TC + 1


BATCH_GROUPS = groups_before(NI)
BATCH_DIAGONALS = diagonals_upto(BATCH_GROUPS - 1)
HEAD_UNITS = sum(len(max_units(n)) for n in range(4))
BATCH_UNITS = sum(len(max_units(n)) for n in range(NI)) + NC * OUT_UNITS
assert BATCH_GROUPS % P_SLOTS == 0 and BATCH_UNITS % 2 == 0 and HEAD_UNITS % 2 == 0


def kept_buffers(nc, ctx):
    def sb(name, shape, dt=F32):
        return ctx.enter_context(nc.sbuf_tensor("kept_" + name, shape, dt))

    return {"ident": sb("ident", [P, P]), "identb": sb("identb", [P, P], BF16),
            "future": sb("future", [P, P], BF16),
            "woh": sb("woh", [P, KE, E], F32R), "wol": sb("wol", [P, KE, E], F32R),
            "qs": sb("qs", [P, H // 2, S], F32R),
            "ks": sb("ks", [P, 2, KV, S], F32R),
            "vv": sb("vv", [P, KV, TT, 2 * D]),
            "group_in": [ctx.enter_context(nc.semaphore(f"kept_group_in{g}")) for g in range(KV)]}


ROWS_TILE = 2


def rows_follow(b, n):
    return not (isinstance(b, int) and b == B - 1 and n == NI - 1)


def batch_steps(engine, prologue, step, epilogue):
    prologue()
    for n in range(2):
        step(0, n, True, False)
    with engine.Fori(0, B - 1) as b:
        for n in range(2, NI + 2):
            step(b, n, True, True)
    for n in range(2, NI):
        step(B - 1, n, n + LOOKAHEAD < NI, True)
    epilogue()


def phase_a2(nc, scratch, kept, x1):
    with ExitStack() as ctx:
        def sb(name, shape, dt=F32):
            return ctx.enter_context(nc.sbuf_tensor("t_" + name, shape, dt))

        def sem(name):
            return ctx.enter_context(nc.semaphore("t_" + name))

        ident, identb, future, woh, wol, qs, ks, vv, group_in = (kept[n] for n in
            ("ident", "identb", "future", "woh", "wol", "qs", "ks", "vv", "group_in"))
        pr = sb("pr", [P, P_SLOTS, G, CW])
        mx = sb("mx", [P, NC, TC, G])
        mm = sb("mm", [P, 2, TC, G])
        mt = sb("mt", [G, 2, CW], F32R)
        ot = sb("ot", [P, 2, CW])
        rc = sb("rc", [P, 2, CW // (2 * D)])
        nm = sb("nm", [P, NC, CW])
        at = sb("at", [P, NC, CW])
        ah, al = sb("ah", [P, KE, S], F32R), sb("al", [P, KE, S], F32R)
        xr = sb("xr", [P, TT, E])
        ps = ctx.enter_context(nc.psum_tensor("t_ps", [P, 8, CW], F32))
        BANKS_S, BANK_O = (4, 5, 7), 6

        passed = {e: sem("passed_" + e) for e in ("sp", "pe", "dve", "pool")}
        xr_in = [sem(f"xr_in{c}") for c in range(NC)]
        unit_ready, unit_done = sem("unit_ready"), sem("unit_done")
        mm_done, mt_ready, mt_done = sem("mm_done"), sem("mt_ready"), sem("mt_done")
        shift_in = [sem(f"shift_in{i}") for i in range(2)]
        score_ready, exp_done, causal_done, pv_done = sem("score_ready"), sem("exp_done"), sem("causal_done"), sem("pv_done")
        norm, at_done, ah_done, al_done = sem("norm"), sem("at_done"), sem("ah_done"), sem("al_done")
        x1_out = [sem(f"x1_out{c}") for c in range(NC)]

        def unit_scores(unit, width):
            bank = 2 * (unit % 2)
            if 2 * width <= CW:
                return ps[:, bank, 0:2 * width].rearrange("p (h k) -> p h k", h=2)
            return ps[:, bank:bank + 2, 0:width]

        def score_bank(u):
            return BANKS_S[u % len(BANKS_S)]

        def rows_block(n):
            return G * (groups_before(n) + ROWS_TILE) + G - 1

        def body_units(b):
            return HEAD_UNITS + b * BATCH_UNITS

        class Count:
            unit = 0

        def out_units_upto(c, h):
            count = 0
            for n in range(2, NI + 2):
                for _, _, item, u in step_units(n, True, True):
                    count += 1
                    if item is None and u == (c, h):
                        return count

        def last_units_upto(c, h):
            count = 0
            for n in range(2, NI):
                for _, _, item, u in step_units(n, n + LOOKAHEAD < NI, True):
                    count += 1
                    if item is None and u == (c, h):
                        return count
            return count + h + 1

        block = ctx.enter_context(nc.Block())

        @block.sync
        def _(sp):
            def load_xr(b, c):
                sp.dma_start(xr[:, TC * c:TC * c + TC, :], scratch["xr"][b, c].rearrange("(t p) e -> p t e", p=P))\
                  .then_inc(xr_in[c], 16)

            def store_x1(b, c, units):
                wait_alone(sp, passed["sp"], unit_done, body_units(b) + units)
                sp.dma_start(x1[NC * b + c].rearrange("(t p) e -> p t e", p=P),
                             xr[:, TC * c:TC * c + TC, :]).then_inc(x1_out[c], 16)

            def shift_rows(b, n):
                g, c = ITEMS[n % NI]
                wait_alone(sp, passed["sp"], mt_done, b * NI + n + 1)
                for half in range(2):
                    sp.dma_start(f32(qs[SHIFT + half:SHIFT + half + 1, 2 * g:2 * g + 2, c * CW:c * CW + CW]),
                                 f32(mt[2 * half:2 * half + 2, n % 2, :])).then_inc(shift_in[n % 2], 16)

            def step(b, n, ahead, out):
                last = isinstance(b, int) and b == B - 1
                if rows_follow(b, n):
                    shift_rows(b, n + 1)
                if n >= 2 and not last:
                    g = (n - 2) // 2
                    wait_alone(sp, passed["sp"], pv_done, b * BATCH_GROUPS + groups_before(2 * g + 2))
                    load_group(sp, scratch, qs, ks, vv, b + 1, g, group_in, n % 2)
                if n == NI - 1:
                    store_x1(b, 0, last_units_upto(0, OUT_UNITS - 1) if last else out_units_upto(0, OUT_UNITS - 1))
                if n == NI + 1:
                    store_x1(b, 1, out_units_upto(1, OUT_UNITS - 1))
                    wait_alone(sp, passed["sp"], x1_out[0], (b + 1) * 16)
                    load_xr(b + 1, 0)
                    wait_alone(sp, passed["sp"], x1_out[1], (b + 1) * 16)
                    load_xr(b + 1, 1)

            def prologue():
                for g in range(1, KV):
                    for part in range(2):
                        load_group(sp, scratch, qs, ks, vv, 0, g, group_in, part)
                for c in range(NC):
                    load_xr(0, c)
                shift_rows(0, 0)

            def epilogue():
                store_x1(B - 1, 1, last_units_upto(1, OUT_UNITS - 1))

            batch_steps(sp, prologue, step, epilogue)
            for c in range(NC):
                sp.wait_ge(x1_out[c], B * 16)

        @block.gpsimd
        def _(pool):
            def attention_lo(b, n):
                if n % 4 < 2:
                    return
                m, c = (n % NI) // 4, n % 2
                pool.wait_ge(ah_done, b * 4 + (n // 4) * 2 + c + 1)
                nc.gpsimd.tensor_tensor(al[:, m, c * CW:c * CW + CW], at[:, c, :], f32(ah[:, m, c * CW:c * CW + CW]),
                                        ALU.subtract).then_inc(al_done, 1)

            def step(b, n, ahead, out):
                for j, (kt, off, diagonal) in enumerate(key_tiles(n)):
                    k = groups_before(n) + j
                    if diagonal:
                        wait_alone(pool, passed["pool"], exp_done, (b * BATCH_GROUPS + k + 1) * G)
                        d = pr[:, k % P_SLOTS, :, off:off + P]
                        nc.gpsimd.affine_select(out=d, in_=d, compare_op=ALU.is_ge, fill=0.0, base=0,
                                                pattern=[[0, G], [1, P]], channel_multiplier=-1)\
                          .then_inc(causal_done, 1)
                    if n and j == hi_lo_after(n):
                        attention_lo(b, n - 1)

            batch_steps(pool, lambda: None, step, lambda: attention_lo(B - 1, NI - 1))

        @block.scalar
        def _(act):
            def shift_row(b, n):
                act.wait_ge(mt_ready, b * NI + n + 1)
                bank = score_bank(rows_block(n - 1)) if n else BANKS_S[0]
                nc.scalar.activation(mt[:, n % 2, :], ps[0:G, bank, :], ACT.Copy, scale=-1.0).then_inc(mt_done, 1)

            def attention_hi(b, n):
                if n % 4 < 2:
                    return
                m, c = (n % NI) // 4, n % 2
                act.wait_ge(at_done, b * 4 + (n // 4) * 2 + c + 3)
                nc.scalar.activation(ah[:, m, c * CW:c * CW + CW], at[:, c, :], ACT.Copy).then_inc(ah_done, 1)

            def step(b, n, ahead, out):
                for j, (kt, off, diagonal) in enumerate(key_tiles(n)):
                    k = groups_before(n) + j
                    if later(b) or k >= P_SLOTS:
                        act.wait_ge(pv_done, b * BATCH_GROUPS + k - P_SLOTS + 1)
                    for i in range(G):
                        if G * k + i == rows_block(n) and rows_follow(b, n):
                            shift_row(b, n + 1)
                        act.wait_ge(score_ready, (b * BATCH_GROUPS + k) * G + i + 1)
                        nc.scalar.activation(pr[:, k % P_SLOTS, i, off:CW], ps[:, score_bank(G * k + i), off:CW],
                                             ACT.Exp, scale=float(D) ** -0.5).then_inc(exp_done, 1)
                    if n and j == hi_lo_after(n):
                        attention_hi(b, n - 1)

            batch_steps(act, lambda: shift_row(0, 0), step, lambda: attention_hi(B - 1, NI - 1))

        @block.tensor
        def _(pe):
            count = Count()

            def slot_free(b):
                if later(b) or count.unit >= 2:
                    pe.wait_ge(unit_done, unit_base(b) + count.unit - 1)

            def unit_base(b):
                return b * BATCH_UNITS

            def max_unit(b, n, qt, pair, k0, width):
                g, c = ITEMS[n % NI]
                if (qt, pair, k0) == (0, 0, 0):
                    pe.wait_ge(group_in[g], (b + n // NI + 1) * GROUP_LOADS)
                slot_free(b)
                diagonal = k0 + width == (qt + 1) * P
                scores = unit_scores(count.unit, width)
                one_bank = diagonal and 2 * width <= CW
                for half in range(2):
                    mm_ = nc.tensor.matmul(scores[:, half, :], qs[0:PAIR, 2 * g + pair, qt * P:qt * P + P],
                                           ks[0:PAIR, half, g, k0:k0 + width],
                                           start=not (one_bank and half), stop=not diagonal)
                    if diagonal and not one_bank:
                        mm_ = nc.tensor.matmul(scores[:, half, width - P:width], identb[:, :], future[:, :],
                                               start=False, stop=True)
                if one_bank:
                    mm_ = nc.tensor.matmul(scores[:, :, width - P:width], identb[:, :],
                                           future[:, None, :].to_broadcast([P, 2, P]), start=False, stop=True)
                mm_.then_inc(unit_ready, 1)
                count.unit += 1

            def out_unit(b, c, h):
                if h == 0:
                    pe.wait_ge(al_done, b * 4 + 2 + c + 3)
                slot_free(b)
                for i in range(2):
                    t = TC * c + 2 * h + i
                    r = slice(t * P, t * P + P)
                    for k in range(KE):
                        mm_ = three(nc, ps[:, 2 * (count.unit % 2) + i, 0:E], ah[:, k, r], al[:, k, r],
                                    woh[:, k, :], wol[:, k, :], k == 0, k == KE - 1)
                mm_.then_inc(unit_ready, 1)
                count.unit += 1

            def max_rows(b, n):
                bank = BANKS_S[0]
                if n:
                    bank = score_bank(rows_block(n - 1))
                    pe.wait_ge(exp_done, b * BATCH_GROUPS * G + rows_block(n - 1) - len(BANKS_S) + 1)
                pe.wait_ge(mm_done, b * NI + n + 1)
                for t in range(TC):
                    mm_ = nc.tensor.transpose(ps[0:G, bank, t * P:t * P + P], mm[:, n % 2, t, :], ident[:, :])
                mm_.then_inc(mt_ready, 1)

            def weigh(b, k):
                n, j = group_at(k)
                g, c = ITEMS[n % NI]
                kt, off, diagonal = key_tiles(n)[j]
                if j == 0 and (later(b) or n):
                    pe.wait_ge(norm, (b * NI + n - 1) * NORM + 2)
                if diagonal:
                    pe.wait_ge(causal_done, b * BATCH_DIAGONALS + diagonals_upto(k))
                else:
                    pe.wait_ge(exp_done, (b * BATCH_GROUPS + k + 1) * G)
                for i in range(G):
                    mm_ = nc.tensor.matmul(ps[32 * i:32 * i + 32, BANK_O, off:CW], vv[:, g, kt, :],
                                           pr[:, k % P_SLOTS, i, off:CW],
                                           start=(j == 0), stop=(j == len(key_tiles(n)) - 1))
                mm_.then_inc(pv_done, 1)

            def prologue():
                for n in range(LOOKAHEAD):
                    for u in max_units(n):
                        max_unit(0, n, *u)
                max_rows(0, 0)

            def step(b, n, ahead, out):
                if n == 2:
                    count.unit = HEAD_UNITS
                g, c = ITEMS[n % NI]
                units = step_units(n, ahead, out)
                pe.wait_ge(shift_in[n % 2], (b * (NI // 2) + n // 2 + 1) * 32)
                for j, (kt, off, diagonal) in enumerate(key_tiles(n)):
                    k = groups_before(n) + j
                    for i in range(G):
                        u = G * k + i
                        if (u == rows_block(n) and rows_follow(b, n)) or (not later(b) and u == 0):
                            pe.wait_ge(mt_done, b * NI + n + (2 if u else 1))
                        elif later(b) or u >= len(BANKS_S):
                            pe.wait_ge(exp_done, b * BATCH_GROUPS * G + u - len(BANKS_S) + 1)
                        nc.tensor.matmul(ps[:, score_bank(u), off:CW], ks[0:ROWS, i % 2, g, kt * P:kt * P + P],
                                         qs[0:ROWS, 2 * g + i // 2, c * CW + off:c * CW + CW],
                                         start=True, stop=True).then_inc(score_ready, 1)
                        if u + 1 == rows_block(n) and rows_follow(b, n):
                            max_rows(b, n + 1)
                        if i == 2 and k >= LAG:
                            weigh(b, k - LAG)
                        while units and units[0][0:2] == (j, i):
                            _, _, item, unit = units.pop(0)
                            if item is None:
                                out_unit(b, *unit)
                            else:
                                max_unit(b, item, *unit)

            def epilogue():
                for k in range(BATCH_GROUPS - LAG, BATCH_GROUPS):
                    weigh(B - 1, k)
                for h in range(OUT_UNITS):
                    out_unit(B - 1, 1, h)

            batch_steps(pe, prologue, step, epilogue)

        @block.vector
        def _(dve):
            dve.sem_inc(norm, 1)
            dve.sem_inc(at_done, 2)
            dve.sem_inc(al_done, 2)
            count = Count()

            def max_unit(b, n, qt, pair, k0, width):
                c = n % 2
                if (qt, pair, k0) == (TC * c, 0, 0) and (later(b) or n >= 2):
                    dve.wait_ge(mt_ready, b * NI + n - 1)
                dve.wait_ge(unit_ready, b * BATCH_UNITS + count.unit + 1)
                dst = mx[:, k0 // CW, qt % TC, pair::2] if c else mm[:, n % 2, qt % TC, pair::2]
                nc.vector.tensor_reduce(dst, unit_scores(count.unit, width), AX_X, ALU.max).then_inc(unit_done, 1)
                count.unit += 1
                if (qt, pair, k0) != (TC * c + TC - 1, 1, CW * c):
                    return
                dve.wait_ge(unit_done, b * BATCH_UNITS + count.unit)
                if c:
                    nc.vector.tensor_tensor(mm[:, n % 2, :, :], mx[:, 0, :, :], mx[:, 1, :, :], ALU.max).then_inc(mm_done, 1)
                else:
                    dve.sem_inc(mm_done, 1)

            def out_unit(b, c, h):
                dve.wait_ge(unit_ready, b * BATCH_UNITS + count.unit + 1)
                dve.wait_ge(xr_in[c], (b + 1) * 16)
                t = TC * c + 2 * h
                nc.vector.tensor_tensor(xr[:, t:t + 2, :], ps[:, 2 * (count.unit % 2):2 * (count.unit % 2) + 2, 0:E],
                                        xr[:, t:t + 2, :], ALU.add).then_inc(unit_done, 1)
                count.unit += 1

            def normalise(b, n):
                g, c = ITEMS[n % NI]
                base = (b * NI + n) * NORM + 1
                o = ot[:, c, :].rearrange("p (k r) -> p k r", r=2 * D)
                dve.wait_ge(pv_done, b * BATCH_GROUPS + groups_before(n + 1))
                dve.wait_ge(norm, base)
                nc.vector.transpose(ot[:, c, :], ps[:, BANK_O, :]).then_inc(norm, 1)
                dve.wait_ge(norm, base + 1)
                nc.vector.reciprocal(rc[:, c, :], o[:, :, D]).then_inc(norm, 1)
                dve.wait_ge(norm, base + 2)
                dve.wait_ge(at_done, b * 4 + (n // 4) * 2 + c + 1)
                nc.vector.tensor_tensor(nm[:, c, :].rearrange("p (k r) -> p k r", r=2 * D)[:, :, D * (g % 2):D * (g % 2) + D],
                                        o[:, :, 0:D], rc[:, c, :, None].to_broadcast([P, CW // (2 * D), D]), ALU.mult)\
                  .then_inc(norm, 1)
                if g % 2:
                    dve.wait_ge(norm, base + 3)
                    dve.wait_ge(al_done, b * 4 + (n // 4) * 2 + c + 1)
                    nc.vector.transpose(at[:, c, :], nm[:, c, :]).then_inc(at_done, 1)

            def prologue():
                for n in range(LOOKAHEAD):
                    for u in max_units(n):
                        max_unit(0, n, *u)

            def step(b, n, ahead, out):
                if n == 2:
                    count.unit = HEAD_UNITS
                waiting = n > 0
                for j, i, item, unit in step_units(n, ahead, out):
                    if waiting and j >= LAG:
                        normalise(b, n - 1)
                        waiting = False
                    if item is None:
                        out_unit(b, *unit)
                    else:
                        max_unit(b, item, *unit)
                if waiting:
                    normalise(b, n - 1)

            def epilogue():
                normalise(B - 1, NI - 1)
                for h in range(OUT_UNITS):
                    out_unit(B - 1, 1, h)

            batch_steps(dve, prologue, step, epilogue)



CHUNKS = B * NC
DFF, MLP = 1024, 2048
MU, MF = DFF // P, MLP // P
RMS_EPS = 1.1920929e-07
CUM_EPS = 1e-6
BLOCK_ROWS = 32 // 2
GU_SLICES = 2 * MLP // CW
DN_SLICES = MF // 2 * E // CW
NIBBLES = 2
DQ_DVE = 7


def load_codes(sp, packed, scales, codes, scale_rows, sem):
    sp.dma_start(codes, packed).then_inc(sem, 16)
    for a in range(P // BLOCK_ROWS):
        sp.dma_start(scale_rows[a * BLOCK_ROWS:(a + 1) * BLOCK_ROWS], scales[a:a + 1].to_broadcast([BLOCK_ROWS, CW]))\
          .then_inc(sem, 16)


LOADS = 16 * (1 + P // BLOCK_ROWS)


def dequantize(nc, dve, codes, scale_rows, bits, mag, out, done, before, nibbles=range(NIBBLES)):
    for e in nibbles:
        at = before + e * DQ_DVE
        m, b = mag[:, e, :], bits[:, e, :]
        nc.vector.tensor_scalar(b, codes, 4 * e, 7, ALU.logical_shift_right, ALU.bitwise_and).then_inc(done, 1)
        dve.wait_ge(done, at + 1)
        nc.vector.tensor_scalar(m.bitcast(I32), b, float(1 << 22), float(126 << 23), ALU.mult, ALU.add).then_inc(done, 1)
        dve.wait_ge(done, at + 2)
        nc.vector.tensor_scalar(b.bitcast(F32), m, 2.0, -1.0, ALU.mult, ALU.add).then_inc(done, 1)
        dve.wait_ge(done, at + 3)
        nc.vector.tensor_tensor(m, m, b.bitcast(F32), ALU.min).then_inc(done, 1)
        dve.wait_ge(done, at + 4)
        nc.vector.tensor_scalar(b, codes, 28 - 4 * e, -(1 << 31), ALU.logical_shift_left, ALU.bitwise_and).then_inc(done, 1)
        nc.vector.tensor_tensor(m, m, scale_rows, ALU.mult).then_inc(done, 1)
        dve.wait_ge(done, at + 6)
        nc.vector.tensor_tensor(out[:, e, :].bitcast(I32), m.bitcast(I32), b, ALU.bitwise_or).then_inc(done, 1)



Y_SIGNALS = 7


def chunk_steps(engine, body):
    body(0, 0, True, False, True)
    with engine.Fori(0, B - 1) as b:
        body(2 * b + 1, 1, True, True, True)
        body(2 * b + 2, 0, True, True, True)
    body(CHUNKS - 1, 1, True, True, False)
    body(CHUNKS, 0, False, True, False)


def phase_b1(nc, x1, w_qkv, w_swiglu, w_out, gu_codes, gu_scales, guh, gul, att):
    with ExitStack() as ctx:
        def sb(name, shape, dt=F32):
            return ctx.enter_context(nc.sbuf_tensor("b_" + name, shape, dt))

        def sem(name):
            return ctx.enter_context(nc.semaphore("b_" + name))

        qkvh, qkvl = sb("qkvh", [P, KE, 3 * E], F32R), sb("qkvl", [P, KE, 3 * E], F32R)
        swh, swl = sb("swh", [P, KE, 2 * DFF], F32R), sb("swl", [P, KE, 2 * DFF], F32R)
        woh, wol = sb("woh", [P, MU, E], F32R), sb("wol", [P, MU, E], F32R)
        xh, xl = sb("xh", [P, KE, CW], F32R), sb("xl", [P, KE, CW], F32R)
        yh, yl = sb("yh", [P, KE, CW], F32R), sb("yl", [P, KE, CW], F32R)
        F_RING = 4
        fh, fl = sb("fh", [P, F_RING, CW], F32R), sb("fl", [P, F_RING, CW], F32R)
        arena = sb("arena", [P, 22 * CW])

        def part(first, n):
            return arena[:, first * CW:(first + n) * CW].rearrange("p (a t) -> p a t", t=CW)

        xb = part(0, 2).rearrange("p a t -> p (a t)").rearrange("p (t e) -> p t e", e=E)
        kk, qq, vv = part(2, 2), part(4, 2), part(6, 2)
        wc, kc = part(8, 2), part(10, 2)
        sqk, sqq = wc, kc
        rk, rq = part(12, 1), part(13, 1)
        sg = part(14, 2)
        ao = part(16, 2)
        bits, mag = part(18, 2).bitcast(I32), part(20, 2)
        codes = sb("codes", [P, CW], I32)
        scale_rows = sb("scale_rows", [P, CW])
        ones = sb("ones", [P, CW])
        mean = sb("mean", [P, P])
        ident = sb("ident", [P, P])
        stats = sb("stats", [P, TC, 6])
        mv = sb("mv", [P, TC, 2])
        s1, s2, half = sb("s1", [P, TC]), sb("s2", [P, TC]), sb("half", [P, TC])
        eps = sb("eps", [P, 1])
        carry = sb("carry", [P, 2, KE])
        raws = [arena[:, first * CW:first * CW + tiles * columns].rearrange("p (k n) -> p k n", k=tiles)
                for first, tiles, columns in ((2, KE, 3 * E), (14, MU, E), (14, KE, 2 * DFF))]
        ps = ctx.enter_context(nc.psum_tensor("b_ps", [P, 8, CW], F32))
        BANK_UG, BANK_OUT = 2, 6

        passed = {e: sem("passed_" + e) for e in ("sp", "dve", "pool")}
        w_in = [sem(f"w_in{i}") for i in range(3)]
        w_hi, qkv_lo, w_lo = sem("w_hi"), sem("qkv_lo"), sem("w_lo")
        fixed = sem("fixed")
        x_in = sem("x_in")
        ln, ln_pool = sem("ln"), sem("ln_pool")
        xt_ready, xh_done, xl_done = sem("xt_ready"), sem("xh_done"), sem("xl_done")
        qkv_ready = sem("qkv_ready")
        kq_copied, squared, v_copied = sem("kq_copied"), sem("squared"), sem("v_copied")
        sq_added = sem("sq_added")
        ms_ready = sem("ms_ready")
        rms_ln, rms_done = sem("rms_ln"), sem("rms_done")
        scaled = sem("scaled")
        exp_done = sem("exp_done")
        wv_done, scan_done, carried = sem("wv_done"), sem("scan_done"), sem("carried")
        quotient = sem("quotient")
        yh_done, yl_done = sem("yh_done"), sem("yl_done")
        ug_ready, silu_done, f_done = sem("ug_ready"), sem("silu_done"), sem("f_done")
        fh_done, fl_done = sem("fh_done"), sem("fl_done")
        summed = sem("summed")
        ao_done, ao_out = sem("ao_done"), sem("ao_out")
        codes_in, dq, gh_done, gl_done = sem("codes_in"), sem("dq"), sem("gh_done"), sem("gl_done")

        block = ctx.enter_context(nc.Block())

        @block.sync
        def _(sp):
            def load_x(ch):
                sp.dma_start(xb, x1[ch].rearrange("(t p) e -> p t e", p=P)).then_inc(x_in, 16)

            def load_gate(ch):
                load_codes(sp, gu_codes[ch], gu_scales[ch], codes[:, :], scale_rows, codes_in)

            load_x(0)
            for i, w in enumerate((w_qkv, w_out, w_swiglu)):
                if i == 2:
                    sp.wait_ge(w_lo, 1)
                sp.dma_start(raws[i], w.rearrange("(k p) n -> p k n", p=P)).then_inc(w_in[i], 16)
                if i == 1:
                    wait_alone(sp, passed["sp"], xt_ready, KE + 1)
                    load_x(1)
                    load_gate(0)

            def body(ch, odd, front, back, ahead, further=True):
                if ahead and further:
                    wait_alone(sp, passed["sp"], xt_ready, (ch + 2) * KE + 1)
                    load_x(ch + 2)
                if front and back:
                    wait_alone(sp, passed["sp"], dq, ch * (NIBBLES * DQ_DVE) + 1)
                    load_gate(ch)
                if back:
                    wait_alone(sp, passed["sp"], ao_done, ch + 1)
                    sp.dma_start(att[ch - 1], ao).then_inc(ao_out, 16)

            body(0, 0, True, False, True)
            with sp.Fori(0, B - 2) as b:
                body(2 * b + 1, 1, True, True, True)
                body(2 * b + 2, 0, True, True, True)
            body(CHUNKS - 3, 1, True, True, True)
            body(CHUNKS - 2, 0, True, True, True, further=False)
            body(CHUNKS - 1, 1, True, True, False)
            body(CHUNKS, 0, False, True, False)
            sp.wait_ge(ao_out, CHUNKS * 16 + 1)

        @block.gpsimd
        def _(pool):
            nc.gpsimd.memset(ident[:, :], 0.0).then_inc(fixed, 1)
            nc.gpsimd.memset(half[:, :], -0.5).then_inc(fixed, 1)
            nc.gpsimd.memset(ones[:, :], 1.0).then_inc(fixed, 1)
            nc.gpsimd.memset(mean[:, :], 1.0 / E).then_inc(fixed, 1)
            nc.gpsimd.memset(eps[:, :], RMS_EPS).then_inc(fixed, 1)
            pool.wait_ge(fixed, 5)
            nc.gpsimd.affine_select(out=ident[:, :], in_=ident[:, :], compare_op=ALU.not_equal, fill=1.0,
                                    base=0, pattern=[[-1, P]], channel_multiplier=1).then_inc(fixed, 1)

            def norm_scales(ch):
                var = mv[:, :, 1]
                chain = [lambda: nc.gpsimd.tensor_scalar(s1[:, :], var, LN_EPS, None, ALU.add),
                         lambda: nc.gpsimd.tensor_tensor(s1[:, :], s1[:, :], half[:, :], ALU.pow),
                         lambda: nc.gpsimd.tensor_tensor(s2[:, :], s1[:, :], s1[:, :], ALU.mult),
                         lambda: nc.gpsimd.tensor_tensor(s2[:, :], s2[:, :], var, ALU.mult),
                         lambda: nc.gpsimd.tensor_scalar(s2[:, :], s2[:, :], RMS_EPS, None, ALU.add),
                         lambda: nc.gpsimd.tensor_tensor(s2[:, :], s2[:, :], half[:, :], ALU.pow),
                         lambda: nc.gpsimd.tensor_tensor(s2[:, :], s2[:, :], s1[:, :], ALU.mult)]
                wait_alone(pool, passed["pool"], ln, ch * (3 * TC) + 2 * TC)
                for i, step in enumerate(chain):
                    if i:
                        wait_alone(pool, passed["pool"], ln_pool, ch * 7 + i)
                    step().then_inc(ln_pool, 1)

            def weights_lo(i, lo, hi):
                pool.wait_ge(w_hi, i + 1)
                nc.gpsimd.tensor_tensor(lo[:, :, :], raws[i], f32(hi[:, :, :]), ALU.subtract).then_inc(w_lo, 1)

            def y_lo(ch):
                pool.wait_ge(yh_done, ch + 1)
                nc.gpsimd.tensor_tensor(yl[:, :, :], qq, f32(yh[:, :, :]), ALU.subtract).then_inc(yl_done, 1)

            def gate_lo(ch):
                pool.wait_ge(gh_done, ch + 1)
                nc.gpsimd.tensor_tensor(gul[:, ch, :, :], mag, f32(guh[:, ch, :, :]), ALU.subtract).then_inc(gl_done, 1)

            def f_lo(ch, j):
                pool.wait_ge(fh_done, ch * MU + j + 1)
                nc.gpsimd.tensor_tensor(fl[:, j % F_RING, :], sg[:, j % 2, :], f32(fh[:, j % F_RING, :]), ALU.subtract)\
                  .then_inc(fl_done, 1)

            def body(ch, odd, front, back, ahead):
                if ahead:
                    norm_scales(ch + 1)
                if not back:
                    weights_lo(2, swl, swh)
                if back:
                    for j in range(MU):
                        f_lo(ch - 1, j)
                if front:
                    y_lo(ch)
                if back:
                    gate_lo(ch - 1)

            norm_scales(0)
            weights_lo(1, wol, woh)
            chunk_steps(pool, body)

        @block.scalar
        def _(act):
            def weights_hi(i, hi):
                act.wait_ge(w_in[i], 16)
                nc.scalar.activation(hi[:, :, :], raws[i], ACT.Copy).then_inc(w_hi, 1)

            def x_hi(ch):
                for k in range(KE):
                    act.wait_ge(xt_ready, ch * KE + k + 2)
                    nc.scalar.activation(xh[:, k, :], ps[:, k, :], ACT.Copy).then_inc(xh_done, 1)

            def project(ch):
                for j in range(2 * KE):
                    dst, sq = (kk, sqk) if j < KE else (qq, sqq)
                    act.wait_ge(qkv_ready, ch * (3 * KE) + j + 1)
                    if j == KE and later(ch):
                        act.wait_ge(yl_done, ch)
                    nc.scalar.activation(dst[:, j % KE, :], ps[:, j % 2, :], ACT.Copy).then_inc(kq_copied, 1)
                    nc.scalar.activation(sq[:, j % KE, :], ps[:, j % 2, :], ACT.Square).then_inc(squared, 1)

            def exponentials(ch):
                for i, r in enumerate((rk, rq)):
                    act.wait_ge(ms_ready, ch * 2 + i + 1)
                    nc.scalar.activation(r, ps[:, BANK_UG + i:BANK_UG + i + 1, :], ACT.Ln, bias=eps[:, :]).then_inc(rms_ln, 1)
                for i, r in enumerate((rk, rq)):
                    act.wait_ge(rms_ln, ch * 2 + i + 1)
                    nc.scalar.activation(r, r, ACT.Exp, scale=-0.5).then_inc(rms_done, 1)
                for i, (t, scale) in enumerate(((kk, 1.0), (qq, -1.0))):
                    act.wait_ge(scaled, ch * 2 + i + 1)
                    nc.scalar.activation(t, t, ACT.Exp, scale=scale).then_inc(exp_done, 1)

            def y_hi(ch):
                act.wait_ge(quotient, (ch + 1) * Y_SIGNALS)
                nc.scalar.activation(yh[:, :, :], qq, ACT.Copy).then_inc(yh_done, 1)

            def silu(ch, j):
                act.wait_ge(ug_ready, ch * MU + j + 1)
                if j >= 2:
                    act.wait_ge(fl_done, ch * MU + j - 1)
                nc.scalar.activation(sg[:, j % 2, :], ps[:, BANK_UG + 2 * (j % 2) + 1, :], ACT.Silu).then_inc(silu_done, 1)

            def f_hi(ch, j):
                act.wait_ge(f_done, ch * MU + j + 3)
                if j >= F_RING:
                    act.wait_ge(summed, ch * MU + j - F_RING + 1)
                nc.scalar.activation(fh[:, j % F_RING, :], sg[:, j % 2, :], ACT.Copy).then_inc(fh_done, 1)

            def sums_out(ch):
                act.wait_ge(summed, (ch + 1) * MU)
                act.wait_ge(ao_out, ch * 16 + 1)
                nc.scalar.activation(ao, ps[:, BANK_OUT:BANK_OUT + KE, :], ACT.Copy).then_inc(ao_done, 1)

            def body(ch, odd, front, back, ahead):
                if front:
                    project(ch)
                    exponentials(ch)
                if back:
                    for j in range(MU):
                        if j:
                            f_hi(ch - 1, j - 1)
                        silu(ch - 1, j)
                        if ahead and j == 2:
                            x_hi(ch + 1)
                    f_hi(ch - 1, MU - 1)
                else:
                    x_hi(ch + 1)
                    weights_hi(2, swh)
                if front:
                    y_hi(ch)
                if back:
                    sums_out(ch - 1)

            weights_hi(0, qkvh)
            x_hi(0)
            weights_hi(1, woh)
            chunk_steps(act, body)

        @block.tensor
        def _(pe):
            def turn(ch):
                pe.wait_ge(ln, (ch + 1) * (3 * TC))
                if later(ch):
                    pe.wait_ge(squared, ch * (2 * KE))
                for k in range(KE):
                    for t in range(TC):
                        mm = nc.tensor.transpose(ps[:, k, t * P:t * P + P], xb[:, t, k * P:k * P + P], ident[:, :])
                    mm.then_inc(xt_ready, 1)

            def project(ch):
                for j, w in enumerate((E, E + P, 0, P, 2 * E, 2 * E + P)):
                    bank = j % 2 if j < 2 * KE else BANK_OUT + j - 2 * KE
                    if j == 0:
                        pe.wait_ge(xl_done, ch * KE + KE)
                    elif KE <= j < 2 * KE:
                        pe.wait_ge(squared, ch * (2 * KE) + j - 1)
                    elif j == 2 * KE and later(ch):
                        pe.wait_ge(ao_done, ch)
                    for k in range(KE):
                        mm = three(nc, ps[:, bank, :], qkvh[:, k, w:w + P], qkvl[:, k, w:w + P],
                                   xh[:, k, :], xl[:, k, :], k == 0, k == KE - 1)
                    mm.then_inc(qkv_ready, 1)
                    if j in (2 * KE - 1, 2 * KE):
                        mean_square(ch, j - 2 * KE + 1)

            def mean_square(ch, i):
                if i == 0 and later(ch):
                    pe.wait_ge(f_done, ch * MU - MU + 2)
                pe.wait_ge(sq_added, ch * 2 + i + 1)
                nc.tensor.matmul(ps[:, BANK_UG + i, :], mean[:, :], (sqk, sqq)[i][:, 0, :], start=True, stop=True)\
                  .then_inc(ms_ready, 1)

            def up_gate(ch, j):
                if j == 0:
                    pe.wait_ge(yl_done, ch + 1)
                pe.wait_ge(f_done, ch * MU + j + 1)
                for i in range(2):
                    w = i * DFF + j * P
                    for k in range(KE):
                        mm = three(nc, ps[:, BANK_UG + 2 * (j % 2) + i, :], swh[:, k, w:w + P], swl[:, k, w:w + P],
                                   yh[:, k, :], yl[:, k, :], k == 0, k == KE - 1)
                mm.then_inc(ug_ready, 1)

            def sum_out(ch, j):
                pe.wait_ge(fl_done, ch * MU + j + 1)
                if j == 0:
                    pe.wait_ge(ao_done, ch + 1)
                for i in range(KE):
                    mm = three(nc, ps[:, BANK_OUT + i, :], woh[:, j, i * P:i * P + P], wol[:, j, i * P:i * P + P],
                               fh[:, j % F_RING, :], fl[:, j % F_RING, :], j == 0, j == MU - 1)
                mm.then_inc(summed, 1)

            def body(ch, odd, front, back, ahead):
                if front:
                    project(ch)
                if not back:
                    turn(ch + 1)
                    return
                if front:
                    pe.wait_ge(rms_ln, (ch + 1) * 2)
                pe.wait_ge(w_hi, 3)
                pe.wait_ge(w_lo, 2)
                for j in range(MU):
                    up_gate(ch - 1, j)
                    if j == 2 and front:
                        pe.wait_ge(v_copied, (ch + 1) * KE)
                    if j >= 2:
                        sum_out(ch - 1, j - 2)
                    if ahead and j == 1:
                        turn(ch + 1)
                for j in (MU - 2, MU - 1):
                    sum_out(ch - 1, j)

            pe.wait_ge(fixed, 6)
            turn(0)
            pe.wait_ge(w_hi, 1)
            pe.wait_ge(qkv_lo, 1)
            chunk_steps(pe, body)

        @block.vector
        def _(dve):
            dve.sem_inc(xt_ready, 1)
            dve.sem_inc(dq, 1)
            dve.sem_inc(gl_done, 1)
            dve.sem_inc(ao_done, 1)
            dve.sem_inc(f_done, 2)
            dve.sem_inc(ao_out, 1)
            dve.wait_ge(fixed, 6)

            def weights_lo(lo, hi):
                dve.wait_ge(w_hi, 1)
                nc.vector.tensor_tensor(lo[:, :, :], raws[0], f32(hi[:, :, :]), ALU.subtract).then_inc(qkv_lo, 1)

            def statistics(ch):
                dve.wait_ge(x_in, ch * 16 + 16)
                for t in range(TC):
                    nc.vector.bn_stats(stats[:, t, :], xb[:, t, :]).then_inc(ln, 1)
                wait_alone(dve, passed["dve"], ln, ch * (3 * TC) + TC)
                for t in range(TC):
                    nc.vector.bn_aggr(mv[:, t, :], stats[:, t, :]).then_inc(ln, 1)

            def normalise(ch):
                dve.wait_ge(ln, ch * (3 * TC) + 2 * TC)
                dve.wait_ge(ln_pool, ch * 7 + 7)
                for t in range(TC):
                    nc.vector.tensor_scalar(xb[:, t, :], xb[:, t, :], mv[:, t, 0:1], s2[:, t:t + 1],
                                            ALU.subtract, ALU.mult).then_inc(ln, 1)

            def x_lo(ch):
                for k in range(KE):
                    dve.wait_ge(xh_done, ch * KE + k + 1)
                    nc.vector.tensor_tensor(xl[:, k, :], ps[:, k, :], f32(xh[:, k, :]), ALU.subtract).then_inc(xl_done, 1)

            def add_squares(ch):
                for i, sq in enumerate((sqk, sqq)):
                    dve.wait_ge(squared, ch * (2 * KE) + (i + 1) * KE)
                    nc.vector.tensor_tensor(sq[:, 0, :], sq[:, 0, :], sq[:, 1, :], ALU.add).then_inc(sq_added, 1)

            def copy_v(ch):
                for k in range(KE):
                    dve.wait_ge(qkv_ready, ch * (3 * KE) + 2 * KE + k + 1)
                    nc.vector.tensor_copy(vv[:, k, :], ps[:, BANK_OUT + k, :]).then_inc(v_copied, 1)

            def scale(ch):
                for i, (t, r) in enumerate(((kk, rk), (qq, rq))):
                    dve.wait_ge(rms_done, ch * 2 + i + 1)
                    dve.wait_ge(kq_copied, ch * (2 * KE) + 2 * i + 2)
                    nc.vector.tensor_tensor(t, t, r.to_broadcast([P, KE, CW]), ALU.mult).then_inc(scaled, 1)

            def cumulate(ch, odd, i):
                src, dst = ((kk, wc), (vv, kc))[i]
                if i == 0:
                    dve.wait_ge(exp_done, ch * 2 + 1)
                    dve.wait_ge(ms_ready, ch * 2 + 2)
                    if odd:
                        dve.wait_ge(carried, ch + 1)
                else:
                    dve.wait_ge(v_copied, ch * KE + KE)
                    nc.vector.tensor_tensor(vv, vv, kk, ALU.mult).then_inc(wv_done, 1)
                    dve.wait_ge(wv_done, ch + 1)
                for k in range(KE):
                    nc.vector.tensor_tensor_scan(dst[:, k, :], ones[:, :], src[:, k, :],
                                                 carry[:, i, k:k + 1] if odd else 0.0, ALU.mult, ALU.add)\
                      .then_inc(scan_done, 1)

            def denominator(ch, odd):
                dve.wait_ge(exp_done, ch * 2 + 2)
                nc.vector.tensor_scalar(qq, qq, 1.0, None, ALU.add).then_inc(quotient, 1)
                dve.wait_ge(scan_done, (ch + 1) * (2 * KE))
                if not odd:
                    for i, s in enumerate((wc, kc)):
                        nc.vector.tensor_copy(carry[:, i, :], s[:, :, CW - 1]).then_inc(carried, 1)
                dve.wait_ge(quotient, ch * Y_SIGNALS + 1)
                nc.vector.scalar_tensor_tensor(qq, wc, CUM_EPS, qq, ALU.add, ALU.mult).then_inc(quotient, 1)

            def reciprocal(ch, quarter):
                if quarter == 0:
                    dve.wait_ge(quotient, ch * Y_SIGNALS + 2)
                q = qq[:, quarter // 2, (quarter % 2) * (CW // 2):(quarter % 2 + 1) * (CW // 2)]
                nc.vector.reciprocal(q, q).then_inc(quotient, 1)

            def gated(ch):
                dve.wait_ge(quotient, ch * Y_SIGNALS + 6)
                nc.vector.tensor_tensor(qq, kc, qq, ALU.mult).then_inc(quotient, 1)

            def gate_values(ch, nibble):
                if nibble == 0:
                    dve.wait_ge(codes_in, (ch + 1) * LOADS)
                    dve.wait_ge(gl_done, ch + 1)
                dequantize(nc, dve, codes[:, :], scale_rows[:, :], bits, mag, mag, dq, ch * (NIBBLES * DQ_DVE) + 1, [nibble])

            def gate_hi(ch):
                dve.wait_ge(dq, (ch + 1) * (NIBBLES * DQ_DVE) + 1)
                nc.vector.tensor_copy(guh[:, ch, :, :], mag).then_inc(gh_done, 1)

            def times_up(ch, j):
                dve.wait_ge(silu_done, ch * MU + j + 1)
                nc.vector.tensor_tensor(sg[:, j % 2, :], ps[:, BANK_UG + 2 * (j % 2), :], sg[:, j % 2, :], ALU.mult)\
                  .then_inc(f_done, 1)

            def body(ch, odd, front, back, ahead):
                def f(j):
                    if back:
                        times_up(ch - 1, j)

                if ahead:
                    statistics(ch + 1)
                if front:
                    add_squares(ch)
                if ahead:
                    normalise(ch + 1)
                if front:
                    copy_v(ch)
                    scale(ch)
                f(0)
                if front:
                    cumulate(ch, odd, 0)
                f(1)
                if front:
                    cumulate(ch, odd, 1)
                f(2)
                if ahead:
                    x_lo(ch + 1)
                if front:
                    denominator(ch, odd)
                    reciprocal(ch, 0)
                f(3)
                if front:
                    reciprocal(ch, 1)
                    reciprocal(ch, 2)
                f(4)
                if front:
                    reciprocal(ch, 3)
                    gated(ch)
                f(5)
                if back:
                    gate_values(ch - 1, 0)
                f(6)
                f(7)
                if back:
                    gate_values(ch - 1, 1)
                    gate_hi(ch - 1)

            statistics(0)
            normalise(0)
            weights_lo(qkvl, qkvh)
            x_lo(0)
            chunk_steps(dve, body)



def mlp_steps(engine, front, both, back):
    front(0, 0)
    both(1, 1, True)
    with engine.Fori(0, B - 1) as b:
        both(2 * b + 2, 0, False)
        both(2 * b + 3, 1, False)
    back(CHUNKS - 1, 1)


def phase_b2(nc, x1, att, guh, gul, dn_codes, dn_scales, out):
    with ExitStack() as ctx:
        def sb(name, shape, dt=F32):
            return ctx.enter_context(nc.sbuf_tensor("c_" + name, shape, dt))

        def sem(name):
            return ctx.enter_context(nc.semaphore("c_" + name))

        TD = MF // NIBBLES
        TS_ = CW // E
        dnh, dnl = sb("dnh", [P, TD, NIBBLES, E], F32R), sb("dnl", [P, TD, NIBBLES, E], F32R)
        xh, xl = sb("xh", [P, 2, KE, CW], F32R), sb("xl", [P, 2, KE, CW], F32R)
        F_RING = 4
        fh, fl = sb("fh", [P, F_RING, CW], F32R), sb("fl", [P, F_RING, CW], F32R)
        gg = sb("gg", [P, F_RING, CW])
        xb = sb("xb", [P, TC, E])
        xn = sb("xn", [P, TC, NIBBLES, P])
        rr = sb("rr", [P, 2, TC, E])
        ab = sb("ab", [P, 2, KE, CW])
        ot = sb("ot", [P, KE, CW])
        oo = sb("oo", [P, TC, E])
        codes = sb("codes", [P, 2, CW], I32)
        scale_rows = sb("scale_rows", [P, 2, CW])
        bits, mag = sb("bits", [P, NIBBLES, CW], I32), sb("mag", [P, NIBBLES, CW])
        ident = sb("ident", [P, P])
        stats = sb("stats", [P, TC, 6])
        mv = sb("mv", [P, TC, 2])
        rstd, half = sb("rstd", [P, TC]), sb("half", [P, TC])
        ps = ctx.enter_context(nc.psum_tensor("c_ps", [P, 8, CW], F32))
        BANK_UG, BANK_OUT = 2, 6

        passed = {e: sem("passed_" + e) for e in ("dve", "pool")}
        fixed = sem("fixed")
        codes_in = [sem(f"codes_in{i}") for i in range(2)]
        dq, dh_done, dl_done = sem("dq"), sem("dh_done"), sem("dl_done")
        x_in = sem("x_in")
        ab_in = [sem(f"ab_in{i}") for i in range(2)]
        ln, ln_pool = sem("ln"), sem("ln_pool")
        xt_ready, xh_done, xl_done = sem("xt_ready"), sem("xh_done"), sem("xl_done")
        gu_ready, gelu_done, f_done = sem("gu_ready"), sem("gelu_done"), sem("f_done")
        fh_done, fl_done = sem("fh_done"), sem("fl_done")
        summed, ot_done, oo_ready, oo_done, oo_out = (sem("summed"), sem("ot_done"), sem("oo_ready"),
                                                      sem("oo_done"), sem("oo_out"))

        def down_slice(j):
            return j // 4 + 1 if j % 4 == 2 and j // 4 + 1 < DN_SLICES else 0

        block = ctx.enter_context(nc.Block())

        @block.sync
        def _(sp):
            def load(ch, odd):
                sp.wait_ge(ln_pool, ch * 3 + 1)
                sp.wait_ge(ln, ch * (3 * TC) + 1)
                sp.dma_start(xb[:, :, :], x1[ch].rearrange("(t p) e -> p t e", p=P)).then_inc(x_in, 16)
                sp.wait_ge(ot_done, (ch - 1) * KE + 1)
                sp.dma_start(ab[:, odd, :, :], att[ch]).then_inc(ab_in[odd], 16)

            def store(ch, odd):
                sp.wait_ge(oo_done, (ch + 1) * 2)
                sp.dma_start(out[ch].rearrange("(t p) e -> p t e", p=P), oo[:, :, :]).then_inc(oo_out, 16)

            def load_down(s):
                load_codes(sp, dn_codes[s], dn_scales[s], codes[:, s % 2, :], scale_rows[:, s % 2, :], codes_in[s % 2])

            def front(ch, odd):
                sp.dma_start(xb[:, :, :], x1[0].rearrange("(t p) e -> p t e", p=P)).then_inc(x_in, 16)
                load_down(0)
                sp.dma_start(ab[:, 0, :, :], att[0]).then_inc(ab_in[0], 16)
                load_down(1)

            def both(ch, odd, first):
                load(ch, odd)
                if first:
                    for s in range(2, DN_SLICES):
                        sp.wait_ge(dq, (s - 1) * (NIBBLES * DQ_DVE))
                        load_down(s)
                else:
                    store(ch - 2, odd)

            def back(ch, odd):
                store(ch - 1, 1 - odd)
                store(ch, odd)

            sp.sem_inc(oo_out, 1)
            mlp_steps(sp, front, both, back)
            sp.wait_ge(oo_out, CHUNKS * 16 + 1)

        @block.gpsimd
        def _(pool):
            nc.gpsimd.memset(ident[:, :], 0.0).then_inc(fixed, 1)
            nc.gpsimd.memset(half[:, :], -0.5).then_inc(fixed, 1)
            pool.wait_ge(fixed, 2)
            nc.gpsimd.affine_select(out=ident[:, :], in_=ident[:, :], compare_op=ALU.not_equal, fill=1.0,
                                    base=0, pattern=[[-1, P]], channel_multiplier=1).then_inc(fixed, 1)

            def rstds(ch):
                wait_alone(pool, passed["pool"], ln, ch * (3 * TC) + 2 * TC + 1)
                nc.gpsimd.tensor_scalar(rstd[:, :], mv[:, :, 1], LN_EPS, None, ALU.add).then_inc(ln_pool, 1)
                pool.wait_ge(ln_pool, ch * 3 + 2)
                nc.gpsimd.tensor_tensor(rstd[:, :], rstd[:, :], half[:, :], ALU.pow).then_inc(ln_pool, 1)

            def residual(ch, odd):
                pool.wait_ge(ln, (ch + 1) * (3 * TC) + 1)
                nc.gpsimd.tensor_tensor(rr[:, odd, :, :].rearrange("p t (m e) -> p t m e", e=NIBBLES),
                                        xb[:, :, :].rearrange("p t (m e) -> p t m e", e=NIBBLES),
                                        xn[:, :, :, :].rearrange("p t e m -> p t m e"), ALU.add).then_inc(ln_pool, 1)

            def f_lo(ch, j):
                pool.wait_ge(fh_done, ch * MF + j + 1)
                nc.gpsimd.tensor_tensor(fl[:, j % F_RING, :], gg[:, j % F_RING, :], f32(fh[:, j % F_RING, :]), ALU.subtract)\
                  .then_inc(fl_done, 1)

            def down_lo(s):
                pool.wait_ge(dh_done, s + 1)
                r = slice(TS_ * s, TS_ * s + TS_)
                nc.gpsimd.tensor_tensor(dnl[:, r, :, :], mag[:, :, :].rearrange("p e (t n) -> p t e n", t=TS_),
                                        f32(dnh[:, r, :, :]), ALU.subtract).then_inc(dl_done, 1)

            def front(ch, odd):
                rstds(ch)
                down_lo(0)
                residual(ch, odd)

            def back(ch, odd):
                for j in range(MF):
                    f_lo(ch, j)

            def both(ch, odd, first):
                for j in range(MF):
                    f_lo(ch - 1, j)
                    if j == 2:
                        rstds(ch)
                    if j == 6:
                        residual(ch, odd)
                    if first and down_slice(j):
                        down_lo(down_slice(j))

            mlp_steps(pool, front, both, back)

        @block.scalar
        def _(act):
            def x_hi(ch, odd, k):
                act.wait_ge(xt_ready, ch * KE + k + 1)
                nc.scalar.activation(xh[:, odd, k, :], ps[:, k, :], ACT.Copy).then_inc(xh_done, 1)

            def gelu(ch, j):
                act.wait_ge(gu_ready, ch * MF + j + 1)
                if j >= F_RING:
                    act.wait_ge(fl_done, ch * MF + j - F_RING + 1)
                nc.scalar.activation(gg[:, j % F_RING, :], ps[:, BANK_UG + 2 * (j % 2), :], ACT.Gelu_apprx_tanh)\
                  .then_inc(gelu_done, 1)

            def f_hi(ch, j):
                act.wait_ge(f_done, ch * MF + j + 3)
                if j >= F_RING:
                    act.wait_ge(summed, ch * MF + j - F_RING + 1)
                nc.scalar.activation(fh[:, j % F_RING, :], gg[:, j % F_RING, :], ACT.Copy).then_inc(fh_done, 1)

            def front(ch, odd):
                for k in range(KE):
                    x_hi(ch, odd, k)
                down_hi(0)

            def down_hi(s):
                act.wait_ge(dq, (s + 1) * (NIBBLES * DQ_DVE))
                nc.scalar.activation(dnh[:, TS_ * s:TS_ * s + TS_, :, :],
                                     mag[:, :, :].rearrange("p e (t n) -> p t e n", t=TS_), ACT.Copy).then_inc(dh_done, 1)

            def all_tiles(ch, between):
                for j in range(MF + 1):
                    if j:
                        f_hi(ch, j - 1)
                    if j < MF:
                        gelu(ch, j)
                    between(j)

            def back(ch, odd):
                all_tiles(ch, lambda j: None)

            def both(ch, odd, first):
                def between(j):
                    if 9 <= j < 9 + KE:
                        x_hi(ch, odd, j - 9)
                    if first and down_slice(j):
                        down_hi(down_slice(j))

                all_tiles(ch - 1, between)

            mlp_steps(act, front, both, back)

        @block.tensor
        def _(pe):
            def x_turn(ch):
                pe.wait_ge(ln, (ch + 1) * (3 * TC) + 1)
                if not isinstance(ch, int):
                    pe.wait_ge(oo_done, (ch - 1) * 2)
                for k in range(NIBBLES):
                    for t in range(TC):
                        mm = nc.tensor.transpose(ps[:, k, t * P:t * P + P], xn[:, t, k, :], ident[:, :])
                    mm.then_inc(xt_ready, 1)

            def gate_up(ch, odd, j):
                if j == 0:
                    pe.wait_ge(xl_done, (ch + 1) * KE)
                pe.wait_ge(f_done, ch * MF + j + 1)
                for i in range(2):
                    s, c = (i * MF + j) // TC, (j % TC) * P
                    for k in range(NIBBLES):
                        mm = three(nc, ps[:, BANK_UG + 2 * (j % 2) + i, :], guh[:, s, k, c:c + P], gul[:, s, k, c:c + P],
                                   xh[:, odd, k, :], xl[:, odd, k, :], k == 0, k == NIBBLES - 1)
                mm.then_inc(gu_ready, 1)

            def sum_out(ch, j):
                pe.wait_ge(fl_done, ch * MF + j + 1)
                if j == 0:
                    pe.wait_ge(ot_done, ch * KE + 1)
                if j % (NIBBLES * TS_) == 0:
                    pe.wait_ge(dl_done, j // (NIBBLES * TS_) + 1)
                for i in range(KE):
                    w = slice(i * P, i * P + P)
                    mm = three(nc, ps[:, BANK_OUT + i, :], dnh[:, j // 2, j % 2, w], dnl[:, j // 2, j % 2, w],
                               fh[:, j % F_RING, :], fl[:, j % F_RING, :], j == 0, j == MF - 1)
                mm.then_inc(summed, 1)

            def out_turn(ch):
                pe.wait_ge(ot_done, (ch + 1) * KE + 1)
                for t in range(TC):
                    for k in range(KE):
                        mm = nc.tensor.transpose(ps[:, t // 2, (t % 2) * E + k * P:(t % 2) * E + k * P + P],
                                                 ot[:, k, t * P:t * P + P], ident[:, :])
                    if t % 2:
                        mm.then_inc(oo_ready, 1)

            LAG = 2

            def all_tiles(ch, odd, between):
                for j in range(MF + LAG):
                    if j < MF:
                        gate_up(ch, odd, j)
                    if j == 1 and later(ch):
                        out_turn(ch - 1)
                    if j >= LAG:
                        sum_out(ch, j - LAG)
                    between(j)

            def back(ch, odd):
                all_tiles(ch, odd, lambda j: None)
                out_turn(ch)

            def both(ch, odd, first):
                all_tiles(ch - 1, 1 - odd, lambda j: x_turn(ch) if j == 8 else None)

            pe.wait_ge(fixed, 3)
            mlp_steps(pe, lambda ch, odd: x_turn(ch), both, back)

        @block.vector
        def _(dve):
            dve.sem_inc(ln, 1)
            dve.sem_inc(ln_pool, 1)
            dve.sem_inc(f_done, 2)
            dve.sem_inc(ot_done, 1)

            def normalise(ch):
                dve.wait_ge(x_in, ch * 16 + 16)
                for t in range(TC):
                    nc.vector.bn_stats(stats[:, t, :], xb[:, t, :]).then_inc(ln, 1)
                wait_alone(dve, passed["dve"], ln, ch * (3 * TC) + TC + 1)
                for t in range(TC):
                    nc.vector.bn_aggr(mv[:, t, :], stats[:, t, :]).then_inc(ln, 1)
                dve.wait_ge(ln, ch * (3 * TC) + 2 * TC + 1)

            def scale_rows_of(ch):
                dve.wait_ge(ln_pool, ch * 3 + 3)
                for t in range(TC):
                    nc.vector.tensor_scalar(xn[:, t, :, :], xb[:, t, :].rearrange("p (m e) -> p e m", e=NIBBLES),
                                            mv[:, t, 0:1], rstd[:, t:t + 1], ALU.subtract, ALU.mult).then_inc(ln, 1)

            def x_lo(ch, odd, k):
                dve.wait_ge(xh_done, ch * KE + k + 1)
                nc.vector.tensor_tensor(xl[:, odd, k, :], ps[:, k, :], f32(xh[:, odd, k, :]), ALU.subtract).then_inc(xl_done, 1)

            def times_up(ch, j):
                dve.wait_ge(gelu_done, ch * MF + j + 1)
                nc.vector.tensor_tensor(gg[:, j % F_RING, :], ps[:, BANK_UG + 2 * (j % 2) + 1, :], gg[:, j % F_RING, :], ALU.mult)\
                  .then_inc(f_done, 1)

            def add_attention(ch, odd):
                dve.wait_ge(summed, (ch + 1) * MF)
                dve.wait_ge(ab_in[odd], (ch - odd + 2) * 8)
                for k in range(KE):
                    nc.vector.tensor_tensor(ot[:, k, :], ps[:, BANK_OUT + k, :], ab[:, odd, k, :], ALU.add).then_inc(ot_done, 1)

            def add_residual(ch, odd):
                for i in range(2):
                    dve.wait_ge(oo_ready, ch * 2 + i + 1)
                    if i == 0:
                        dve.wait_ge(oo_out, ch * 16 + 1)
                        dve.wait_ge(ln_pool, ch * 3 + 4)
                    nc.vector.tensor_tensor(oo[:, 2 * i:2 * i + 2, :], ps[:, i, :].rearrange("p (t e) -> p t e", e=E),
                                            rr[:, odd, 2 * i:2 * i + 2, :], ALU.add).then_inc(oo_done, 1)

            def down_values(s, nibble):
                if nibble == 0:
                    dve.wait_ge(codes_in[s % 2], (s // 2 + 1) * LOADS)
                    if s:
                        dve.wait_ge(dl_done, s)
                dequantize(nc, dve, codes[:, s % 2, :], scale_rows[:, s % 2, :], bits, mag, mag, dq, s * (NIBBLES * DQ_DVE), [nibble])

            def front(ch, odd):
                normalise(ch)
                scale_rows_of(ch)
                for k in range(KE):
                    x_lo(ch, odd, k)
                for nibble in range(NIBBLES):
                    down_values(0, nibble)

            def all_tiles(ch, odd, between):
                for j in range(MF):
                    times_up(ch, j)
                    if j == 1 and later(ch):
                        add_residual(ch - 1, 1 - odd)
                    between(j)
                add_attention(ch, odd)

            def both(ch, odd, first):
                def between(j):
                    if j == 2:
                        normalise(ch)
                    if j == 5:
                        scale_rows_of(ch)
                    if 9 <= j < 9 + KE:
                        x_lo(ch, odd, j - 9)
                    if first and j % 4 < NIBBLES and j // 4 + 1 < DN_SLICES:
                        down_values(j // 4 + 1, j % 4)

                all_tiles(ch - 1, 1 - odd, between)

            def back(ch, odd):
                all_tiles(ch, odd, lambda j: None)
                add_residual(ch, odd)

            mlp_steps(dve, front, both, back)

def build(nc, d):
    x1 = nc.dram_tensor("x1_scratch", [CHUNKS, CW, E], F32, kind="Internal").ap()
    att = nc.dram_tensor("att_scratch", [CHUNKS, P, KE, CW], F32, kind="Internal").ap()
    def scratch_tensor(name, shape):
        return nc.dram_tensor(name + "_scratch", shape, F32, kind="Internal").ap()

    scratch = {"q": scratch_tensor("q", [B, 2, E, S]), "k": scratch_tensor("k", [B, 2, KV * D, S]),
               "v": scratch_tensor("v", [B, NC, P, KV, TC, 2 * D]), "xr": scratch_tensor("xr", [B, NC, CW, E])}
    with ExitStack() as ctx:
        kept = kept_buffers(nc, ctx)
        phase_a1(nc, d["x"], d["w0"], d["w_bin"], d["bias_cols"], d["bias_rows"], d["rope"], scratch, kept)
        phase_a2(nc, scratch, kept, x1)
    with ExitStack() as ctx:
        guh, gul = (ctx.enter_context(nc.sbuf_tensor(name, [P, GU_SLICES, NIBBLES, CW], F32R)) for name in ("guh", "gul"))
        phase_b1(nc, x1, d["w_qkv"], d["w_swiglu"], d["w_out"], d["gu_codes"], d["gu_scales"], guh, gul, att)
        phase_b2(nc, x1, att, guh, gul, d["dn_codes"], d["dn_scales"], d["out"])


def rope_tables():
    inv = (1.0 / np.float32(10000.0) ** (np.arange(0, D, 2, dtype=np.float32) / np.float32(D))).astype(np.float32)
    angle = np.arange(S, dtype=np.float32)[None, :] * inv[np.arange(P) % (D // 2)][:, None]
    sign = np.where(np.arange(P) % D < D // 2, -1.0, 1.0).astype(np.float32)[:, None]
    return np.stack([np.cos(angle), np.sin(angle) * sign]).astype(np.float32)


def swap_halves(a):
    return np.roll(a.reshape(-1, D, *a.shape[1:]), D // 2, axis=1).reshape(a.shape)


def gate_columns(a):
    rows = a.shape[0]
    a = a.reshape(rows, MLP // (NIBBLES * P), P, NIBBLES).transpose(0, 1, 3, 2).reshape(rows, MLP // CW, CW)
    return a.transpose(1, 0, 2)


def down_slices(a, rows):
    return a.reshape(DN_SLICES, CW // E, rows, E).transpose(0, 2, 1, 3).reshape(DN_SLICES, rows, CW)


def lay_out(i):
    wq, wk, bq, bk = i["L0_attn_wq"], i["L0_attn_wk"], i["L0_attn_bq"], i["L0_attn_bk"]
    wo = i["L0_attn_wo"].T.reshape(KV // 2, 2, G, D, E).transpose(0, 2, 1, 3, 4).reshape(E, E)
    bqr, bkr = swap_halves(bq), swap_halves(bk)
    return {
        "x": i["L0_attn_x"].reshape(B * NC, CW, E),
        "w0": np.concatenate([wq.T, swap_halves(wq).T, wk.T, i["L0_attn_wv"].T, swap_halves(wk).T, wo], axis=1),
        "w_bin": i["L0_ffn_weight"],
        "bias_cols": np.stack([bq[:P], bq[P:], bqr[:P], bqr[P:], np.concatenate([bk, i["L0_attn_bv"]]),
                               np.concatenate([bkr, bkr])], axis=1),
        "bias_rows": np.stack([i["L0_attn_bo"], i["L0_ffn_bias"]]),
        "rope": rope_tables(),
        "w_qkv": i["L1_attn_w_qkv"].T,
        "w_swiglu": i["L1_attn_w_swiglu"].T,
        "w_out": i["L1_attn_w_out"].T,
        "gu_codes": np.concatenate([gate_columns(i["L1_ffn_gate_W_packed"].T), gate_columns(i["L1_ffn_up_W_packed"].T)]),
        "gu_scales": np.concatenate([gate_columns(i["L1_ffn_gate_scales"].T), gate_columns(i["L1_ffn_up_scales"].T)]),
        "dn_codes": down_slices(i["L1_ffn_down_W_packed"].T, P),
        "dn_scales": down_slices(i["L1_ffn_down_scales"].T, P // BLOCK_ROWS),
    }


def kernel(**inputs):
    import concourse.bacc as bacc
    from concourse.bass_utils import run_bass_kernel_spmd

    nc = bacc.Bacc("TRN2", target_bir_lowering=False, num_devices=1)
    arrays, dram = {}, {}
    for name, a in lay_out({k: np.asarray(v) for k, v in inputs.items()}).items():
        arrays[f"in_{name}"] = np.ascontiguousarray(a)
        dram[name] = nc.dram_tensor(f"in_{name}", a.shape, mybir.dt.from_np(a.dtype), kind="ExternalInput").ap()
    dram["out"] = nc.dram_tensor("out_0", (CHUNKS, CW, E), F32, kind="ExternalOutput").ap()
    build(nc, dram)
    r = run_bass_kernel_spmd(nc, [arrays], core_ids=[0])
    return r.results[0]["out_0"].reshape(B, S, E)
```
